# Optimizing a Trainium2 kernel written in Bass

```python
import numpy as np
import jax
import jax.numpy as jnp

def _softmax(x, axis=-1):
    return jax.nn.softmax(x, axis=axis)
def _gelu(x):
    return jax.nn.gelu(x, approximate=True)
def _silu(x):
    return jax.nn.silu(x)
def _sigmoid(x):
    return jax.nn.sigmoid(x)
def _layernorm(x, axis=-1, eps=1e-5):
    m = jnp.mean(x, axis=axis, keepdims=True)
    v = jnp.var(x, axis=axis, keepdims=True)
    return (x - m) / jnp.sqrt(v + eps)
def _scatter_add(tgt, idx, src, axis=0):
    return tgt.at[idx].add(src)
def _segment_sum(src, seg, n):
    return jax.ops.segment_sum(src, seg, n)

kernel_name = 'mk_adj_preln_d1_adj_512_03c6d8'

def setup_inputs(seed: int = 0):
    np.random.seed(seed)
    _w = jnp.asarray
    def _rec_inputs():
        import jax
        import jax.numpy as jnp
        _gk = jax.random.key(seed)
        x = 7.34e-05 + 1 * jax.random.normal(jax.random.fold_in(_gk, 1), (16, 1024, 512), jnp.float32)
        _w = (1.0 + jnp.arange(1024, dtype=jnp.float32)) ** -0.5
        _w = _w / _w.mean()
        _pij = jnp.clip(0.015625 * _w[:, None] * _w[None, :], 0.0, 1.0)
        _a = jax.random.uniform(jax.random.fold_in(_gk, 2), (1024, 1024)) < _pij
        _a = jnp.logical_or(_a, jnp.swapaxes(_a, -1, -2))
        _a = jnp.logical_or(_a, jnp.eye(1024, dtype=bool))
        _af = _a.astype(jnp.float32)
        adj = _af
        return x, adj
    x, adj = _rec_inputs()
    def _L0_gnn_setup():
        import jax, jax.numpy as jnp
        import numpy as np
        B, N, D, H = (16, 1025, 512, 8)
        LN_EPS = 1e-05

        def _make_mask(key, n):
            n_proto = n - 1
            adj = jax.random.bernoulli(key, 0.03, (n_proto, n_proto)).astype(jnp.float32)
            adj = jnp.clip(adj + adj.T + jnp.eye(n_proto, dtype=jnp.float32), 0.0, 1.0)
            mask = jnp.zeros((n, n), dtype=jnp.float32)
            mask = mask.at[0, :].set(1.0).at[:, 0].set(1.0)
            mask = mask.at[1:, 1:].set(adj)
            return mask
        key = jax.random.key(seed)
        ks = jax.random.split(key, 7)
        s = 1.0 / np.sqrt(D)
        return {'x': jax.random.normal(ks[0], (B, N, D), dtype=jnp.float32), 'w_qkv': jax.random.uniform(ks[1], (D, 3 * D), dtype=jnp.float32, minval=-s, maxval=s), 'w_proj': jax.random.uniform(ks[2], (D, D), dtype=jnp.float32, minval=-s, maxval=s), 'b_proj': jnp.zeros((D,), dtype=jnp.float32), 'ln_gamma': jnp.ones((D,), dtype=jnp.float32), 'ln_beta': jnp.zeros((D,), dtype=jnp.float32), 'attn_mask': _make_mask(ks[3], N)}
    _L0_gnn_all = _L0_gnn_setup()
    _L0_gnn_in = {k: v for k, v in _L0_gnn_all.items() if k in ('w_qkv', 'w_proj', 'b_proj', 'ln_gamma', 'ln_beta', )}
    del _L0_gnn_all

    return {
        "x": x,
        "adj": adj,
        "L0_gnn_w_qkv": _L0_gnn_in["w_qkv"],
        "L0_gnn_w_proj": _L0_gnn_in["w_proj"],
        "L0_gnn_b_proj": _L0_gnn_in["b_proj"],
        "L0_gnn_ln_gamma": _L0_gnn_in["ln_gamma"],
        "L0_gnn_ln_beta": _L0_gnn_in["ln_beta"],
    }

def reference(x, adj, L0_gnn_w_qkv, L0_gnn_w_proj, L0_gnn_b_proj, L0_gnn_ln_gamma, L0_gnn_ln_beta):
    import jax
    import jax.numpy as jnp
    def _L0_gnn_ref(x, w_qkv, w_proj, b_proj, ln_gamma, ln_beta, attn_mask):
        import jax, jax.numpy as jnp
        import numpy as np
        B, N, D, H = (16, 1025, 512, 8)
        LN_EPS = 1e-05

        def _make_mask(key, n):
            n_proto = n - 1
            adj = jax.random.bernoulli(key, 0.03, (n_proto, n_proto)).astype(jnp.float32)
            adj = jnp.clip(adj + adj.T + jnp.eye(n_proto, dtype=jnp.float32), 0.0, 1.0)
            mask = jnp.zeros((n, n), dtype=jnp.float32)
            mask = mask.at[0, :].set(1.0).at[:, 0].set(1.0)
            mask = mask.at[1:, 1:].set(adj)
            return mask
        b, n, d = x.shape
        hd = d // H
        scale = hd ** (-0.5)
        qkv = (x @ w_qkv).reshape(b, n, 3, H, hd).transpose(2, 0, 3, 1, 4)
        q, k, v = (qkv[0], qkv[1], qkv[2])
        attn = jnp.einsum('bhnd,bhmd->bhnm', q, k) * scale
        attn = jnp.where(attn_mask[None, None] == 0, -jnp.inf, attn)
        attn = jax.nn.softmax(attn, axis=-1)
        o = jnp.einsum('bhnm,bhmd->bhnd', attn, v).transpose(0, 2, 1, 3).reshape(b, n, d)
        o = o @ w_proj + b_proj
        mu = jnp.mean(o, axis=-1, keepdims=True)
        var = jnp.mean(jnp.square(o - mu), axis=-1, keepdims=True)
        ln = (o - mu) * jax.lax.rsqrt(var + LN_EPS) * ln_gamma + ln_beta
        return o + ln

    h = jnp.maximum(_layernorm(x, axis=-1), 0.0)
    x = x + _L0_gnn_ref(h, L0_gnn_w_qkv, L0_gnn_w_proj, L0_gnn_b_proj, L0_gnn_ln_gamma, L0_gnn_ln_beta, adj)
    return x


_drawn_inputs = setup_inputs


def setup_inputs(seed=0):
    import zlib

    import numpy as np

    out = dict(_drawn_inputs(seed))
    spreads = {'L0_gnn_b_proj': (0.0, 0.1), 'L0_gnn_ln_gamma': (1.0, 0.2), 'L0_gnn_ln_beta': (0.0, 0.1)}
    factors = {}
    for name, (base, spread) in spreads.items():
        noise = np.random.default_rng([zlib.crc32(name.encode()), seed]).standard_normal(out[name].shape)
        drawn = base * np.exp(spread * noise) if base else spread * noise
        out[name] = jnp.asarray(drawn.astype(out[name].dtype))
    for name, factor in factors.items():
        out[name] = (out[name] * factor).astype(out[name].dtype)
    return out
```

```python
from contextlib import ExitStack

import numpy as np

import concourse.bass as bass
from concourse import mybir

P = 128
B, N, D = 16, 1024, 512
HEADS = 8
HD = D // HEADS
TILES = N // P
KT = D // P
PAIRS = HEADS // 2
STEPS = 2 * TILES
CHUNKS = TILES // 2
SLOTS = PAIRS * STEPS
HALF = N // 2
XRING = 4

F32 = mybir.dt.float32
F32R = mybir.dt.float32r
F16 = mybir.dt.float16
BF16 = mybir.dt.bfloat16
I32 = mybir.dt.int32
ALU = mybir.AluOpType
ACT = mybir.ActivationFunctionType
AX_X = mybir.AxisListType.X
RMAX = bass.bass_isa.ReduceOp.max

EPS = 1e-5
ATT_SCALE = float(HD) ** -0.5
MASKED = -1e30
HUGE = 3e38
H_SCALE_LOG2 = 8
W_TOP_LOG2 = 13
MANT = 23


PROJ_AT = (1, 3, 6, 9, 11, 14, 17, 19)
HT_AT = (43, 44, 45, 46, 48, 49, 51, 52)
QK_AT = ((53, 55, 59, 62), (4, 8, 12, 21), (23, 25, 27, 33), (37, 39, 41, 42))
V_AT = ((47, 50, 57, 61), (29, 31, 35, 36))

FILL = {}
for t in range(TILES):
    FILL[PROJ_AT[t]] = ("proj", t)
    FILL[HT_AT[t]] = ("ht", t)
for n, slots in enumerate(QK_AT):
    for i, s in enumerate(slots):
        FILL[s] = ("qk", n, i)
for n, slots in enumerate(V_AT):
    for i, s in enumerate(slots):
        FILL[s] = ("v", n, i)
assert len(FILL) == 2 * TILES + 4 * (len(QK_AT) + len(V_AT))


def for_next(unit):
    return unit[0] == "ht" or unit[0] in ("qk", "v") and unit[1] == 0


PREPARE = [FILL[s] for s in sorted(FILL) if for_next(FILL[s])]


def build(nc, x, adj, w_qkv, w_proj, b_proj, gamma, beta, out):
    x_tiles = x.rearrange("b (t p) d -> (b t) p d", p=P)
    out_tiles = out.rearrange("b (t p) d -> (b t) p d", p=P)

    with ExitStack() as ctx:
        def sb(name, shape, dt):
            return ctx.enter_context(nc.sbuf_tensor(name, shape, dt))

        def psum(name, shape, dt):
            return ctx.enter_context(nc.psum_tensor(name, shape, dt))

        def sem(name):
            return ctx.enter_context(nc.semaphore(name))

        mask = sb("mask", [P, TILES, N], BF16)
        w_hi = sb("w_hi", [P, KT, 3 * D], F16)
        w_lo = sb("w_lo", [P, KT, 3 * D], F16)
        w_out = sb("w_out", [P, KT, D], F32)
        bias_b = sb("bias_b", [P, D], F32)
        gamma_b = sb("gamma_b", [P, D], F32)
        beta_b = sb("beta_b", [P, D], F32)
        ident = sb("ident", [P, P], F32)
        ht_hi = sb("ht_hi", [P, KT, N], F16)
        ht_lo = sb("ht_lo", [P, KT, N], F16)
        q_st = sb("q_st", [P, 2, 2, N], F32R)
        k_st = sb("k_st", [P, 2, 2, N], F32R)
        k_sw = sb("k_sw", [P, 2, 2, N], F32R)
        v = sb("v", [P, 2, TILES, 2 * P], F32)
        probs = sb("probs", [P, 2, N], F32)
        pt = sb("pt", [P, 2, 2, TILES, 2 * P], F32)
        ot = sb("ot", [P, PAIRS, N], F32)
        xt = sb("xt", [P, XRING, D], F32)
        o_t = sb("o_t", [P, 2, D], F32)
        norm_t = sb("norm_t", [P, D], F32)
        neg_max = sb("neg_max", [P, 2], F32)
        row_sum = sb("row_sum", [P, 2], F32)
        inv_sum = sb("inv_sum", [P, 2], F32)
        x_st = sb("x_st", [P, 2, 6], F32)
        x_mv = sb("x_mv", [P, 2, 2], F32)
        x_aff = sb("x_aff", [P, 2, 4], F32)
        o_st = sb("o_st", [P, 2, 6], F32)
        o_mv = sb("o_mv", [P, 2, 2], F32)
        o_aff = sb("o_aff", [P, 2, 2], F32)
        minus_half = sb("minus_half", [P, 1], F32)
        minus_one = sb("minus_one", [P, 1], F32)
        eps = sb("eps", [P, 1], F32)
        w_amax = sb("w_amax", [P, 8], F32)
        w_exp = sb("w_exp", [P, 4], I32)
        w_stage = pt[:].rearrange("p a h t n -> p (a h t n)")[:, 0:KT * 3 * D].rearrange(
            "p (k n) -> p k n", k=KT)
        adj_stage = pt[:].rearrange("p a h t n -> p (a h t n)").rearrange("p (t n) -> p t n", t=TILES)
        w_abs = v[:].rearrange("p a t n -> p (a t n)")[:, 0:3 * D].bitcast(I32)

        ps_s = psum("ps_s", [P, 2, N], F32)
        ps_t = psum("ps_t", [P, 2, 4, P], F32)
        ps_o = psum("ps_o", [P, 2 * P], F32)
        ps_f = psum("ps_f", [P, HALF], F32)

        x_loaded = [sem(f"x_loaded{r}") for r in range(XRING)]
        out_stored = [sem(f"out_stored{r}") for r in range(XRING)]
        k_swapped = [sem(f"k_swapped{i}") for i in range(4)]
        w_loaded = sem("w_loaded")
        adj_loaded = sem("adj_loaded")
        w_out_loaded = sem("w_out_loaded")
        bias_loaded = sem("bias_loaded")
        gamma_loaded = sem("gamma_loaded")
        beta_loaded = sem("beta_loaded")
        zeroed = sem("zeroed")
        ident_ready = sem("ident_ready")
        consts_ready = sem("consts_ready")
        w_prep = sem("w_prep")
        w_max_ready = sem("w_max_ready")
        w_ready = sem("w_ready")
        mask_ready = sem("mask_ready")
        scores_ready = sem("scores_ready")
        masked = sem("masked")
        exp_ready = sem("exp_ready")
        inverted = sem("inverted")
        probs_ready = sem("probs_ready")
        transposed = sem("transposed")
        pt_ready = sem("pt_ready")
        heads_ready = sem("heads_ready")
        ot_ready = sem("ot_ready")
        done = {k: sem(f"{k}_done") for k in ("ht", "qk", "v", "proj")}
        high = {k: sem(f"{k}_high") for k in ("ht", "qk")}
        read = {k: sem(f"{k}_read") for k in ("ht", "qk", "v", "proj")}
        x_stats = sem("x_stats")
        x_moments = sem("x_moments")
        x_var = sem("x_var")
        x_neg = sem("x_neg")
        x_dev = sem("x_dev")
        x_affine = sem("x_affine")
        h_ready = sem("h_ready")
        o_stats = sem("o_stats")
        o_moments = sem("o_moments")
        o_var = sem("o_var")
        o_dev = sem("o_dev")
        o_normed = sem("o_normed")
        x_plus_beta = sem("x_plus_beta")
        x_plus_o = sem("x_plus_o")
        o_gamma = sem("o_gamma")
        out_ready = sem("out_ready")
        carried = sem("carried")

        block = ctx.enter_context(nc.Block())

        def count(unit, b):
            if unit[0] == "proj":
                return (b - 1) * TILES + unit[1] + 1
            if unit[0] == "ht":
                return (b + 1) * TILES + unit[1] + 1
            ahead = 1 if unit[1] == 0 else 0
            if unit[0] == "qk":
                return ((b + ahead) * PAIRS + unit[1]) * 4 + unit[2] + 1
            return ((b + ahead) * 2 + unit[1]) * 4 + unit[2] + 1

        def units_of(b, first, last):
            return {s: u for s, u in FILL.items()
                    if not (first and u[0] == "proj") and not (last and for_next(u))}

        def since(eng, signal, n):
            if isinstance(n, int) and n <= 0:
                return
            eng.wait_ge(signal, n)

        def carry_wait():
            nc.vector.sem_inc(carried, 1)

        def ln_load(b, t):
            if isinstance(b, int) and b == 0:
                return t // XRING + 1
            return 4 * b - 2 + t // XRING + 1

        def res_load(b, t):
            if isinstance(b, int) and b == B - 1:
                return 4 * b + 2 + t // XRING + 1
            return 4 * b + 4 + t // XRING + 1

        def stores(b, t):
            return 2 * b + t // XRING + 1

        def run(engine_loop, batch):
            batch(0, True, False)
            with engine_loop(1, B - 1) as b:
                batch(b, False, False)
            batch(B - 1, False, True)

        @block.sync
        def _(sp):
            def load_ln(b, t):
                r = t % XRING
                if t >= XRING:
                    sp.wait_ge(done["ht"], count(("ht", t - XRING), b - 1))
                elif not (isinstance(b, int) and b <= 1):
                    sp.wait_ge(out_stored[r], 16 * stores(b - 2, t + XRING))
                elif b == 1:
                    sp.wait_ge(done["ht"], count(("ht", t + XRING), -1))
                sp.dma_start(xt[:, r, :], x_tiles[b * TILES + t]).then_inc(x_loaded[r], 16)

            def load_res(b, t):
                r = t % XRING
                if t >= XRING or (isinstance(b, int) and b == B - 1):
                    before = stores(b, t - XRING) if t >= XRING else stores(b - 1, t + XRING)
                    sp.wait_ge(out_stored[r], 16 * before)
                else:
                    sp.wait_ge(done["ht"], count(("ht", t + XRING), b))
                sp.dma_start(xt[:, r, :], x_tiles[b * TILES + t]).then_inc(x_loaded[r], 16)

            def store(b, t):
                r = t % XRING
                sp.wait_ge(out_ready, b * TILES + t + 1)
                sp.dma_start(out_tiles[b * TILES + t], xt[:, r, :]).then_inc(out_stored[r], 16)

            def swap(unit, b):
                _, pair, i = unit
                a = pair % 2
                sp.wait_ge(read["qk"], count(unit, b))
                for side in range(2):
                    to = slice(side * HD, side * HD + HD)
                    fro = slice((1 - side) * HD, (1 - side) * HD + HD)
                    keys = slice(i * HALF, (i + 1) * HALF)
                    sp.dma_start(k_sw[to, a, :, keys].bitcast(F32),
                                 k_st[fro, a, :, keys].bitcast(F32)).then_inc(k_swapped[2 * i + side], 16)

            def batch(b, first, last):
                units = units_of(b, first, last)
                for s in range(SLOTS):
                    unit = units.get(s - 1)
                    if unit and unit[0] == "qk" and unit[2] < 2:
                        swap(unit, b)
                    for t in range(TILES):
                        if not first and s == PROJ_AT[t] + 4:
                            store(b - 1, t)
                    for t in range(TILES):
                        if not first and s == max(0, PROJ_AT[t] - 4):
                            load_res(b - 1, t)
                        if not last and s == HT_AT[t] - 4:
                            load_ln(b + 1, t)

            for t in range(XRING):
                sp.dma_start(xt[:, t, :], x_tiles[t]).then_inc(x_loaded[t], 16)
            for row, tile, signal in ((b_proj, bias_b, bias_loaded), (gamma, gamma_b, gamma_loaded),
                                      (beta, beta_b, beta_loaded)):
                sp.dma_start(tile[:], row.rearrange("(a n) -> a n", a=1).broadcast_to([P, D])).then_inc(signal, 16)
            sp.dma_start(w_stage, w_qkv.rearrange("(k p) n -> p k n", p=P)).then_inc(w_loaded, 16)
            sp.wait_ge(w_ready, 2)
            sp.dma_start(adj_stage, adj.rearrange("(t p) n -> p t n", p=P)).then_inc(adj_loaded, 16)
            for t in range(XRING, TILES):
                load_ln(0, t)
            sp.dma_start(w_out[:], w_proj.rearrange("(k p) n -> p k n", p=P)).then_inc(w_out_loaded, 16)
            for unit in PREPARE:
                if unit[0] == "qk" and unit[2] < 2:
                    swap(unit, -1)
            run(sp.Fori, batch)
            for t in range(TILES):
                load_res(B - 1, t)
                if t >= 1:
                    store(B - 1, t - 1)
            store(B - 1, TILES - 1)
            for r in range(XRING):
                sp.wait_ge(out_stored[r], 16 * stores(B - 1, XRING + r))

        @block.tensor
        def _(pe):
            def scores(b, w, s):
                g = b * SLOTS + w * STEPS + s
                a, h, j = w % 2, s % 2, 2 * (s // 4) + s % 4 // 2
                if s == 0:
                    pe.wait_ge(read["qk"], (b * PAIRS + w) * 4 + 3)
                    for i in range(4):
                        pe.wait_ge(k_swapped[i], 16 * (b * PAIRS + w + 1))
                if s == STEPS // 2:
                    pe.wait_ge(read["qk"], (b * PAIRS + w) * 4 + 4)
                since(pe, exp_ready, g - 1)
                for n in range(2):
                    keys = slice(n * HALF, (n + 1) * HALF)
                    q = q_st[:, a, h, j * P:(j + 1) * P]
                    nc.tensor.matmul(ps_s[:, s % 2, keys], q, k_sw[:, a, h, keys], start=True, stop=False)
                    last = nc.tensor.matmul(ps_s[:, s % 2, keys], q, k_st[:, a, h, keys], start=False, stop=True)
                last.then_inc(scores_ready, 1)

            def transposes(g, parity):
                pe.wait_ge(probs_ready, g + 1)
                for half in range(2):
                    since(pe, pt_ready, 2 * g - 1 + half)
                    for i in range(4):
                        t = half * 4 + i
                        last = nc.tensor.transpose(ps_t[:, half, i, :], probs[:, parity, t * P:(t + 1) * P], ident[:])
                    last.then_inc(transposed, 1)

            def values(b, w, c, part):
                n = (b * PAIRS + w) * CHUNKS + c
                if part == 0:
                    pe.wait_ge(pt_ready, 8 * (n + 1))
                    since(pe, ot_ready, n)
                    if c == 0 and w % 2 == 0:
                        pe.wait_ge(read["v"], (b * 2 + w // 2 + 1) * 4)
                for t in (2 * part, 2 * part + 1):
                    for h in range(2):
                        col = (w % 2) * P + h * HD
                        last = nc.tensor.matmul(ps_o[h * HD:(h + 1) * HD, :], v[:, w // 2, t, col:col + HD],
                                                pt[:, c % 2, h, t, :], start=(t == 0), stop=(t == TILES - 1))
                if part == 3:
                    last.then_inc(heads_ready, 1)

            def split_matmuls(dst, stationary, moving):
                n = 0
                for k in range(KT):
                    for sa, mo in ((0, 1), (1, 0), (0, 0)):
                        last = nc.tensor.matmul(dst, stationary(k, sa), moving(k, mo),
                                                start=(n == 0), stop=(n == 3 * KT - 1))
                        n += 1
                return last

            def do(unit, b, before):
                if before:
                    pe.wait_ge(read[before[0][0]], count(*before))
                kind = unit[0]
                w_, h_ = (w_hi, w_lo), (ht_hi, ht_lo)
                if kind == "proj":
                    t = unit[1]
                    pe.wait_ge(ot_ready, ((b - 1) * PAIRS + PAIRS - 1) * CHUNKS + t // 2 + 1)
                    for k in range(KT):
                        last = nc.tensor.matmul(ps_f[:], ot[:, k, t * P:(t + 1) * P], w_out[:, k, :],
                                                start=(k == 0), stop=(k == KT - 1))
                elif kind == "ht":
                    t = unit[1]
                    pe.wait_ge(h_ready, count(unit, b))
                    for k in range(KT):
                        last = nc.tensor.transpose(ps_f[:, k * P:(k + 1) * P],
                                                   xt[:, t % XRING, k * P:(k + 1) * P], ident[:])
                elif kind == "qk":
                    _, pair, i = unit
                    col = (D if i < 2 else 0) + pair * P
                    rows = slice(i % 2 * HALF, (i % 2 + 1) * HALF)
                    last = split_matmuls(ps_f[:], lambda k, part: w_[part][:, k, col:col + P],
                                         lambda k, part: h_[part][:, k, rows])
                else:
                    _, half, i = unit
                    col = 2 * D + half * 2 * P
                    for e in range(2):
                        rows = slice((2 * i + e) * P, (2 * i + e + 1) * P)
                        last = split_matmuls(ps_f[:, e * 2 * P:(e + 1) * 2 * P],
                                             lambda k, part: h_[part][:, k, rows],
                                             lambda k, part: w_[part][:, k, col:col + 2 * P])
                last.then_inc(done[kind], 1)

            def batch(b, first, last):
                units = units_of(b, first, last)
                before = (PREPARE[-1], b - 1)
                for s in range(SLOTS):
                    g = b * SLOTS + s
                    scores(b, s // STEPS, s % STEPS)
                    if s >= 2 or not first:
                        transposes(g - 2, s % 2)
                    c, part = divmod(s - 6, 4)
                    if c >= 0:
                        values(b, c // CHUNKS, c % CHUNKS, part)
                    elif not first:
                        values(b - 1, PAIRS - 1, CHUNKS + c, part)
                    if s in units:
                        do(units[s], b, before)
                        before = (units[s], b)

            pe.wait_ge(ident_ready, 1)
            before = None
            for unit in PREPARE:
                if unit == next(u for u in PREPARE if u[0] != "ht"):
                    pe.wait_ge(w_ready, 2)
                do(unit, -1, before)
                before = (unit, -1)
            pe.wait_ge(w_out_loaded, 16)
            run(pe.Fori, batch)
            for g in range(B * SLOTS - 2, B * SLOTS):
                transposes(g, g % 2)
            for part in (2, 3):
                values(B - 1, PAIRS - 1, CHUNKS - 2, part)
            for part in range(4):
                values(B - 1, PAIRS - 1, CHUNKS - 1, part)
            before = (("qk", PAIRS - 1, 3), B - 1)
            for t in range(TILES):
                do(("proj", t), B, before)
                before = (("proj", t), B)

        @block.vector
        def _(dve):
            def normalise(g, parity):
                dve.wait_ge(exp_ready, g + 1)
                nc.vector.reciprocal(inv_sum[:, parity:parity + 1], row_sum[:, parity:parity + 1]).then_inc(inverted, 1)
                dve.wait_ge(inverted, g + 1)
                nc.vector.tensor_scalar(probs[:, parity, :], probs[:, parity, :], inv_sum[:, parity:parity + 1],
                                        None, ALU.mult).then_inc(probs_ready, 1)

            def mask_and_max(g, s):
                dve.wait_ge(scores_ready, g + 1)
                carry_wait()
                j = 2 * (s // 4) + s % 4 // 2
                nc.vector.tensor_tensor_reduce(ps_s[:, s % 2, :], ps_s[:, s % 2, :], mask[:, j, :], -ATT_SCALE,
                                               HUGE, ALU.add, ALU.min, neg_max[:, s % 2:s % 2 + 1]).then_inc(masked, 1)

            def take(unit, b):
                kind, n = unit[0], count(unit, b)
                dve.wait_ge(done[kind], n)
                if kind == "proj":
                    t = unit[1]
                    dve.wait_ge(x_plus_o, n)
                    nc.vector.tensor_tensor(o_t[:, t % 2, :], ps_f[:], bias_b[:], ALU.add).then_inc(read[kind], 1)
                    dve.wait_ge(read[kind], n)
                    nc.vector.bn_stats(o_st[:, t % 2, :], o_t[:, t % 2, :]).then_inc(o_stats, 1)
                    dve.wait_ge(o_stats, n)
                    carry_wait()
                    nc.vector.bn_aggr(o_mv[:, t % 2, :], o_st[:, t % 2, :]).then_inc(o_moments, 1)
                elif kind == "ht":
                    rows = slice(unit[1] * P, (unit[1] + 1) * P)
                    dve.wait_ge(high[kind], n)
                    nc.vector.scalar_tensor_tensor(
                        out=ht_lo[:, :, rows], in0=ps_f[:].rearrange("p (k n) -> p k n", k=KT),
                        scalar=2.0 ** H_SCALE_LOG2, in1=ht_hi[:, :, rows], op0=ALU.mult,
                        op1=ALU.subtract).then_inc(read[kind], 1)
                elif kind == "qk":
                    _, pair, i = unit
                    dst = k_st if i < 2 else q_st
                    rows = slice(i % 2 * HALF, (i % 2 + 1) * HALF)
                    dve.wait_ge(high[kind], n)
                    for h in range(2):
                        here = slice(h * HD, (h + 1) * HD)
                        there = slice((1 - h) * HD, (1 - h) * HD + HD)
                        last = nc.vector.scalar_tensor_tensor(
                            out=dst[there, pair % 2, h, rows], in0=ps_f[here, :], scalar=w_exp[here, 2:3].bitcast(F32),
                            in1=dst[here, pair % 2, h, rows].bitcast(F32), op0=ALU.mult, op1=ALU.subtract)
                    last.then_inc(read[kind], 1)
                else:
                    _, half, i = unit
                    nc.vector.tensor_scalar(v[:, half, 2 * i:2 * i + 2, :], ps_f[:].rearrange("p (e n) -> p e n", e=2),
                                            w_exp[:, 2:3].bitcast(F32), None, ALU.mult).then_inc(read[kind], 1)

            def standardise(b, t):
                n = b * TILES + t + 1
                dve.wait_ge(o_dev, n)
                since(dve, out_ready, n - 1)
                nc.vector.tensor_scalar(norm_t[:], o_t[:, t % 2, :], o_mv[:, t % 2, 0:1], o_aff[:, t % 2, 1:2],
                                        ALU.subtract, ALU.mult).then_inc(o_normed, 1)

            def x_statistics(b, t):
                n = b * TILES + t + 1
                dve.wait_ge(x_loaded[t % XRING], 16 * ln_load(b, t))
                since(dve, x_affine, n - 2)
                nc.vector.bn_stats(x_st[:, t % 2, :], xt[:, t % XRING, :]).then_inc(x_stats, 1)
                dve.wait_ge(x_stats, n)
                carry_wait()
                nc.vector.bn_aggr(x_mv[:, t % 2, :], x_st[:, t % 2, :]).then_inc(x_moments, 1)

            def batch(b, first, last):
                units = units_of(b, first, last)
                for s in range(SLOTS):
                    g = b * SLOTS + s
                    waited = s - 1 in units and units[s - 1][0] != "ht"
                    if waited:
                        normalise(g - 1, (s - 1) % 2)
                    if s - 1 in units:
                        take(units[s - 1], b)
                    mask_and_max(g, s % STEPS)
                    if not waited and (s >= 1 or not first):
                        normalise(g - 1, (s - 1) % 2)
                    for t in range(TILES):
                        if not first and s == PROJ_AT[t] + 2:
                            standardise(b - 1, t)
                        if not last and s == HT_AT[t] - 2:
                            x_statistics(b + 1, t)

            def power_of_two(step):
                nc.vector.tensor_scalar(w_exp[:, 0:1], w_amax[:, 5:6].bitcast(I32), 0x7F800000, None,
                                        ALU.bitwise_and).then_inc(w_prep, 1)
                dve.wait_ge(w_prep, step + 1)
                nc.vector.tensor_scalar(w_exp[:, 3:4], w_exp[:, 0:1], float(40 << MANT), None,
                                        ALU.max).then_inc(w_prep, 1)
                dve.wait_ge(w_prep, step + 2)
                nc.vector.tensor_scalar(w_exp[:, 1:2], w_exp[:, 3:4], -1.0, float((254 + W_TOP_LOG2) << MANT),
                                        ALU.mult, ALU.add).then_inc(w_prep, 1)
                nc.vector.tensor_scalar(w_exp[:, 2:3], w_exp[:, 3:4], float(-((W_TOP_LOG2 + H_SCALE_LOG2) << MANT)),
                                        None, ALU.add).then_inc(w_prep, 1)
                dve.wait_ge(w_prep, step + 4)

            for t in range(2):
                x_statistics(0, t)
            dve.wait_ge(w_loaded, 16)
            for k in range(KT):
                if k:
                    dve.wait_ge(w_prep, 2 * k)
                nc.vector.tensor_scalar(w_abs, w_stage[:, k, :].bitcast(I32), 0x7FFFFFFF, None,
                                        ALU.bitwise_and).then_inc(w_prep, 1)
                dve.wait_ge(w_prep, 2 * k + 1)
                nc.vector.tensor_reduce(w_amax[:, k:k + 1], w_abs.bitcast(F32), AX_X, ALU.max).then_inc(w_prep, 1)
            dve.wait_ge(w_prep, 2 * KT)
            nc.vector.tensor_reduce(w_amax[:, 4:5], w_amax[:, 0:KT], AX_X, ALU.max).then_inc(w_prep, 1)
            dve.wait_ge(w_max_ready, 1)
            power_of_two(2 * KT + 1)
            nc.vector.tensor_scalar(w_hi[:], w_stage, w_exp[:, 1:2].bitcast(F32), None, ALU.mult).then_inc(w_ready, 1)
            dve.wait_ge(w_ready, 1)
            nc.vector.scalar_tensor_tensor(
                out=w_lo[:].rearrange("p k n -> p (k n)"), in0=w_stage.rearrange("p k n -> p (k n)"),
                scalar=w_exp[:, 1:2].bitcast(F32), in1=w_hi[:].rearrange("p k n -> p (k n)"),
                op0=ALU.mult, op1=ALU.subtract).then_inc(w_ready, 1)
            for unit in PREPARE:
                if unit[0] == "ht" and unit[1] + 2 < TILES:
                    x_statistics(0, unit[1] + 2)
                take(unit, -1)
            dve.wait_ge(adj_loaded, 16)
            nc.vector.tensor_scalar(mask[:], adj_stage, 0.0, MASKED, ALU.is_equal, ALU.mult).then_inc(mask_ready, 1)
            dve.wait_ge(mask_ready, 1)
            dve.wait_ge(bias_loaded, 16)
            run(dve.Fori, batch)
            normalise(B * SLOTS - 1, 1)
            for t in range(TILES + 1):
                if t < TILES:
                    if t >= 2:
                        dve.wait_ge(o_normed, (B - 1) * TILES + t - 1)
                    take(("proj", t), B)
                if t:
                    standardise(B - 1, t - 1)

        @block.scalar
        def _(act):
            def high_part(unit, b):
                kind, n = unit[0], count(unit, b)
                act.wait_ge(done[kind], n)
                if kind == "ht":
                    rows = slice(unit[1] * P, (unit[1] + 1) * P)
                    nc.scalar.activation(ht_hi[:, :, rows], ps_f[:].rearrange("p (k n) -> p k n", k=KT),
                                         ACT.Copy, scale=2.0 ** H_SCALE_LOG2).then_inc(high[kind], 1)
                else:
                    _, pair, i = unit
                    dst = k_st if i < 2 else q_st
                    rows = slice(i % 2 * HALF, (i % 2 + 1) * HALF)
                    for h in range(2):
                        here = slice(h * HD, (h + 1) * HD)
                        last = nc.scalar.activation(dst[here, pair % 2, h, rows], ps_f[here, :], ACT.Copy,
                                                    scale=w_exp[here, 2:3].bitcast(F32))
                    last.then_inc(high[kind], 1)

            def copy_transposed(g, s, n):
                if s % 4 == 0:
                    since(act, heads_ready, n - 1)
                h, c, col = s % 2, s // 4 % 2, s % 4 // 2 * P
                for half in range(2):
                    act.wait_ge(transposed, 2 * g + half + 1)
                    nc.scalar.activation(pt[:, c, h, half * 4:half * 4 + 4, col:col + P], ps_t[:, half, :, :],
                                         ACT.Copy).then_inc(pt_ready, 1)

            def copy_heads(b, w, c):
                act.wait_ge(heads_ready, (b * PAIRS + w) * CHUNKS + c + 1)
                nc.scalar.activation(ot[:, w, c * 2 * P:(c + 1) * 2 * P], ps_o[:],
                                     ACT.Copy).then_inc(ot_ready, 1)

            def exponential(g, parity):
                act.wait_ge(masked, g + 1)
                since(act, transposed, 2 * (g - 1))
                nc.scalar.activation(probs[:, parity, :], ps_s[:, parity, :], ACT.Exp,
                                     bias=neg_max[:, parity:parity + 1], scale=-1.0,
                                     accum_out=row_sum[:, parity:parity + 1]).then_inc(exp_ready, 1)

            def relu_norm(b, t):
                act.wait_ge(x_affine, b * TILES + t + 1)
                nc.scalar.activation(xt[:, t % XRING, :], xt[:, t % XRING, :], ACT.Relu,
                                     bias=x_aff[:, t % 2, 3:4], scale=x_aff[:, t % 2, 1:2]).then_inc(h_ready, 1)

            def batch(b, first, last):
                units = units_of(b, first, last)
                for s in range(SLOTS):
                    g = b * SLOTS + s
                    if s - 1 in units and units[s - 1][0] in ("ht", "qk"):
                        high_part(units[s - 1], b)
                    if s % 4 == 2:
                        c = (s - 10) // 4
                        if c >= 0:
                            copy_heads(b, c // CHUNKS, c % CHUNKS)
                        elif not first:
                            copy_heads(b - 1, PAIRS - 1, CHUNKS + c)
                    if s >= 2 or not first:
                        copy_transposed(g - 2, (s - 2) % STEPS, b * (SLOTS // 4) + (s - 2) // 4)
                    exponential(g, s % 2)
                    for t in range(TILES):
                        if not last and s == HT_AT[t] - 1:
                            relu_norm(b + 1, t)

            relu_norm(0, 0)
            for unit in PREPARE:
                if unit[0] == "ht" and unit[1] + 1 < TILES:
                    relu_norm(0, unit[1] + 1)
                if unit[0] != "v":
                    high_part(unit, -1)
            run(act.Fori, batch)
            for g in range(B * SLOTS - 2, B * SLOTS):
                copy_transposed(g, g % STEPS, g // 4)
            for c in (CHUNKS - 2, CHUNKS - 1):
                copy_heads(B - 1, PAIRS - 1, c)

        @block.gpsimd
        def _(pool):
            def x_scale_and_shift(b, t):
                n, a = b * TILES + t + 1, t % 2
                pool.wait_ge(x_moments, n)
                since(pool, h_ready, n - 2)
                nc.gpsimd.tensor_tensor(x_aff[:, a, 0:1], x_mv[:, a, 1:2], eps[:], ALU.add).then_inc(x_var, 1)
                nc.gpsimd.tensor_tensor(x_aff[:, a, 2:3], x_mv[:, a, 0:1], minus_one[:], ALU.mult).then_inc(x_neg, 1)
                pool.wait_ge(x_var, n)
                nc.gpsimd.tensor_tensor(x_aff[:, a, 1:2], x_aff[:, a, 0:1], minus_half[:], ALU.pow).then_inc(x_dev, 1)
                pool.wait_ge(x_neg, n)
                pool.wait_ge(x_dev, n)
                nc.gpsimd.tensor_tensor(x_aff[:, a, 3:4], x_aff[:, a, 2:3], x_aff[:, a, 1:2],
                                        ALU.mult).then_inc(x_affine, 1)

            def add_beta(b, t):
                n, r = b * TILES + t + 1, t % XRING
                pool.wait_ge(x_loaded[r], 16 * res_load(b, t))
                nc.gpsimd.tensor_tensor(xt[:, r, :], xt[:, r, :], beta_b[:], ALU.add).then_inc(x_plus_beta, 1)

            def finish(b, t):
                n, r, a = b * TILES + t + 1, t % XRING, t % 2
                pool.wait_ge(o_moments, n)
                nc.gpsimd.tensor_tensor(o_aff[:, a, 0:1], o_mv[:, a, 1:2], eps[:], ALU.add).then_inc(o_var, 1)
                pool.wait_ge(o_var, n)
                nc.gpsimd.tensor_tensor(o_aff[:, a, 1:2], o_aff[:, a, 0:1], minus_half[:], ALU.pow).then_inc(o_dev, 1)
                pool.wait_ge(x_plus_beta, n)
                nc.gpsimd.tensor_tensor(xt[:, r, :], xt[:, r, :], o_t[:, a, :], ALU.add).then_inc(x_plus_o, 1)
                pool.wait_ge(o_normed, n)
                nc.gpsimd.tensor_tensor(norm_t[:], norm_t[:], gamma_b[:], ALU.mult).then_inc(o_gamma, 1)
                pool.wait_ge(o_gamma, n)
                pool.wait_ge(x_plus_o, n + 2)
                nc.gpsimd.tensor_tensor(xt[:, r, :], xt[:, r, :], norm_t[:], ALU.add).then_inc(out_ready, 1)

            def batch(b, first, last):
                if not first:
                    add_beta(b - 1, 0)
                    for t in range(TILES):
                        if t + 1 < TILES:
                            add_beta(b - 1, t + 1)
                        finish(b - 1, t)
                if not last:
                    for t in range(TILES):
                        x_scale_and_shift(b + 1, t)

            nc.gpsimd.memset(ident[:], 0.0).then_inc(zeroed, 1)
            for tile, value in ((minus_half, -0.5), (minus_one, -1.0), (eps, EPS)):
                nc.gpsimd.memset(tile[:], value).then_inc(consts_ready, 1)
            for a in range(2):
                nc.gpsimd.memset(o_t[:, a, :], 0.0).then_inc(x_plus_o, 1)
            pool.wait_ge(zeroed, 1)
            nc.gpsimd.affine_select(out=ident[:], in_=ident[:], compare_op=ALU.not_equal, fill=1.0, base=0,
                                    pattern=[[-1, P]], channel_multiplier=1).then_inc(ident_ready, 1)
            pool.wait_ge(consts_ready, 3)
            x_scale_and_shift(0, 0)
            x_scale_and_shift(0, 1)
            pool.wait_ge(w_prep, 2 * KT + 1)
            nc.gpsimd.partition_all_reduce(w_amax[:, 5:6], w_amax[:, 4:5], P, RMAX).then_inc(w_max_ready, 1)
            for t in range(2, TILES):
                x_scale_and_shift(0, t)
            pool.wait_ge(beta_loaded, 16)
            pool.wait_ge(gamma_loaded, 16)
            run(pool.Fori, batch)
            add_beta(B - 1, 0)
            for t in range(TILES):
                if t + 1 < TILES:
                    add_beta(B - 1, t + 1)
                finish(B - 1, t)


INPUTS = ("x", "adj", "L0_gnn_w_qkv", "L0_gnn_w_proj", "L0_gnn_b_proj", "L0_gnn_ln_gamma", "L0_gnn_ln_beta")


def kernel(**inputs):
    import concourse.bacc as bacc
    from concourse.bass_utils import run_bass_kernel_spmd

    nc = bacc.Bacc("TRN2", target_bir_lowering=False, num_devices=1)
    arrays, args = {}, []
    for name in INPUTS:
        a = np.ascontiguousarray(inputs[name])
        arrays[f"in_{name}"] = a
        args.append(nc.dram_tensor(f"in_{name}", a.shape, mybir.dt.from_np(a.dtype), kind="ExternalInput").ap())
    args.append(nc.dram_tensor("out", (B, N, D), F32, kind="ExternalOutput").ap())
    build(nc, *args)
    r = run_bass_kernel_spmd(nc, [arrays], core_ids=[0])
    return r.results[0]["out"]
```

```python
from contextlib import ExitStack

import numpy as np

import concourse.bass as bass
from concourse import mybir

P = 128
B, N, D = 16, 1024, 512
HEADS = 8
HD = D // HEADS
TILES = N // P
KT = D // P
PAIRS = HEADS // 2
STEPS = 2 * TILES
CHUNKS = TILES // 2
SLOTS = PAIRS * STEPS
HALF = N // 2
XRING = 4

F32 = mybir.dt.float32
F16 = mybir.dt.float16
BF16 = mybir.dt.bfloat16
I32 = mybir.dt.int32
ALU = mybir.AluOpType
ACT = mybir.ActivationFunctionType
AX_X = mybir.AxisListType.X
RMAX = bass.bass_isa.ReduceOp.max

EPS = 1e-5
ATT_LOG2_SCALE = 3
assert 4**ATT_LOG2_SCALE == HD
MASKED = -(2.0 ** 126)
HUGE = 3e38
H_SCALE_LOG2 = 8
W_TOP_LOG2 = 13
ATT_LOG2 = -8
OUT_OF_PSUM = 2.0 ** (ATT_LOG2 - H_SCALE_LOG2)
MANT = 23


PROJ_AT = ((0, 1), (2, 3), (5, 6), (7, 8), (12, 13), (14, 15), (16, 17), (18, 19))
HT_AT = ((43,), (44,), (45,), (46,), (48,), (49,), (51,), (52,))
QK_AT = (((53, 54), (55, 56), (59, 60), (62, 63)), ((4,), (9,), (10, 11), (20, 21)),
         ((22, 23), (24, 25), (26, 27), (32, 33)), ((36, 37), (38,), (39, 40), (41, 42)))
V_AT = (((47,), (50,), (57, 58), (61,)), ((28, 29), (30, 31), (34,), (35,)))

UNITS = {("proj", t): slots for t, slots in enumerate(PROJ_AT)}
UNITS |= {("ht", t): slots for t, slots in enumerate(HT_AT)}
UNITS |= {("qk", n, i): slots for n, at in enumerate(QK_AT) for i, slots in enumerate(at)}
UNITS |= {("v", n, i): slots for n, at in enumerate(V_AT) for i, slots in enumerate(at)}
FILL = {s: (unit, i, len(slots)) for unit, slots in UNITS.items() for i, s in enumerate(slots)}
assert len(FILL) == SLOTS == sum(len(slots) for slots in UNITS.values())
ENDS = {slots[-1]: unit for unit, slots in UNITS.items()}


def for_next(unit):
    return unit[0] == "ht" or unit[0] in ("qk", "v") and unit[1] == 0


PREPARE = [ENDS[s] for s in sorted(ENDS) if for_next(ENDS[s])]


def build(nc, x, adj, w_qkv, w_proj, b_proj, gamma, beta, out):
    x_tiles = x.rearrange("b (t p) d -> (b t) p d", p=P)
    out_tiles = out.rearrange("b (t p) d -> (b t) p d", p=P)

    with ExitStack() as ctx:
        def sb(name, shape, dt):
            return ctx.enter_context(nc.sbuf_tensor(name, shape, dt))

        def psum(name, shape, dt):
            return ctx.enter_context(nc.psum_tensor(name, shape, dt))

        def sem(name):
            return ctx.enter_context(nc.semaphore(name))

        mask = sb("mask", [P, TILES, N], BF16)
        w_hi = sb("w_hi", [P, KT, 3 * D], F16)
        w_lo = sb("w_lo", [P, KT, 3 * D], F16)
        wo_hi = sb("wo_hi", [P, KT, D], F16)
        wo_lo = sb("wo_lo", [P, KT, D], F16)
        bias_b = sb("bias_b", [P, D], F32)
        gamma_b = sb("gamma_b", [P, D], F32)
        beta_b = sb("beta_b", [P, D], F32)
        ident = sb("ident", [P, P], F32)
        ht_hi = sb("ht_hi", [P, KT, N], F16)
        ht_lo = sb("ht_lo", [P, KT, N], F16)
        q_st = sb("q_st", [P, 2, 2, N], F16)
        k_st = sb("k_st", [P, 2, 2, N], F16)
        k_sw = sb("k_sw", [P, 2, 2, N], F16)
        v = sb("v", [P, 2, TILES, 2 * P], F32)
        probs = sb("probs", [P, 2, N], F32)
        pt = sb("pt", [P, 2, 2, TILES, 2 * P], F32)
        ot_hi = sb("ot_hi", [P, PAIRS, N], F16)
        ot_lo = sb("ot_lo", [P, PAIRS, N], F16)
        xt = sb("xt", [P, XRING, D], F32)
        o_t = sb("o_t", [P, 2, D], F32)
        norm_t = sb("norm_t", [P, D], F32)
        neg_max = sb("neg_max", [P, 2], F32)
        row_sum = sb("row_sum", [P, 2], F32)
        inv_sum = sb("inv_sum", [P, 2], F32)
        x_st = sb("x_st", [P, 2, 6], F32)
        x_mv = sb("x_mv", [P, 2, 2], F32)
        x_aff = sb("x_aff", [P, 2, 4], F32)
        o_st = sb("o_st", [P, 2, 6], F32)
        o_mv = sb("o_mv", [P, 2, 2], F32)
        o_aff = sb("o_aff", [P, 2, 2], F32)
        minus_half = sb("minus_half", [P, 1], F32)
        minus_one = sb("minus_one", [P, 1], F32)
        eps = sb("eps", [P, 1], F32)
        w_stage = sb("w_stage", [P, KT, 3 * D], F32)
        wo_stage = v[:, 1].rearrange("p t n -> p (t n)").rearrange("p (k n) -> p k n", k=KT)
        w_abs = ot_lo[:].rearrange("p a n -> p (a n)").bitcast(I32)
        w_part = sb("w_part", [P, KT], F32)
        w_top = sb("w_top", [P, 2], F32)
        w_all = sb("w_all", [P, 2], F32)
        top_bits = sb("top_bits", [P, 2], I32)
        clamped_bits = sb("clamped_bits", [P, 2], I32)
        w_scale = sb("w_scale", [P, 2], I32)
        product_bits = sb("product_bits", [P, 2], I32)
        score_scale = sb("score_scale", [P, 1], F32)
        proj_scale = sb("proj_scale", [P, 1], I32)
        adj_stage = pt[:].rearrange("p a h t n -> p (a h t n)").rearrange("p (t n) -> p t n", t=TILES)

        ps_s = psum("ps_s", [P, 2, N], F32)
        ps_t = psum("ps_t", [P, 2, 4, P], F32)
        ps_o = psum("ps_o", [P, 2 * P], F32)
        ps_f = psum("ps_f", [P, HALF], F32)

        spare = [ps_f[:], *(ps_t[:, half].rearrange("p a n -> p (a n)") for half in range(2))]

        x_loaded = [sem(f"x_loaded{r}") for r in range(XRING)]
        out_stored = [sem(f"out_stored{r}") for r in range(XRING)]
        k_swapped = [sem(f"k_swapped{i}") for i in range(4)]
        w_loaded = [sem(f"w_loaded{k}") for k in range(KT)]
        adj_loaded = sem("adj_loaded")
        w_out_loaded = sem("w_out_loaded")
        bias_loaded = sem("bias_loaded")
        gamma_loaded = sem("gamma_loaded")
        beta_loaded = sem("beta_loaded")
        zeroed = sem("zeroed")
        ident_ready = sem("ident_ready")
        consts_ready = sem("consts_ready")
        w_prep = sem("w_prep")
        w_top_ready = sem("w_top_ready")
        w_max_ready = sem("w_max_ready")
        scale_ready = sem("scale_ready")
        w_high = sem("w_high")
        w_ready = sem("w_ready")
        mask_ready = sem("mask_ready")
        scores_ready = sem("scores_ready")
        masked = sem("masked")
        exp_ready = sem("exp_ready")
        inverted = sem("inverted")
        probs_ready = sem("probs_ready")
        transposed = sem("transposed")
        pt_ready = sem("pt_ready")
        heads_ready = sem("heads_ready")
        ot_high = sem("ot_high")
        ot_ready = sem("ot_ready")
        done = {k: sem(f"{k}_done") for k in ("ht", "qk", "v", "proj")}
        high = {k: sem(f"{k}_high") for k in ("ht", "qk")}
        read = {k: sem(f"{k}_read") for k in ("ht", "qk", "v", "proj")}
        x_stats = sem("x_stats")
        x_moments = sem("x_moments")
        x_var = sem("x_var")
        x_neg = sem("x_neg")
        x_dev = sem("x_dev")
        x_affine = sem("x_affine")
        h_ready = sem("h_ready")
        o_stats = sem("o_stats")
        o_moments = sem("o_moments")
        o_var = sem("o_var")
        o_dev = sem("o_dev")
        o_normed = sem("o_normed")
        x_plus_beta = sem("x_plus_beta")
        x_plus_o = sem("x_plus_o")
        o_gamma = sem("o_gamma")
        out_ready = sem("out_ready")
        carried = sem("carried")

        block = ctx.enter_context(nc.Block())

        def count(unit, b):
            if unit[0] == "proj":
                return (b - 1) * TILES + unit[1] + 1
            if unit[0] == "ht":
                return (b + 1) * TILES + unit[1] + 1
            ahead = 1 if unit[1] == 0 else 0
            if unit[0] == "qk":
                return ((b + ahead) * PAIRS + unit[1]) * 4 + unit[2] + 1
            return ((b + ahead) * 2 + unit[1]) * 4 + unit[2] + 1

        def has(unit, first, last):
            return not (first and unit[0] == "proj") and not (last and for_next(unit))

        def ended(s, b, first, last):
            if s == 0:
                return (None, b) if first else (ENDS.get(SLOTS - 1), b - 1)
            unit = ENDS.get(s - 1)
            return (unit if unit and has(unit, first, last) else None), b

        def since(eng, signal, n):
            if isinstance(n, int) and n <= 0:
                return
            eng.wait_ge(signal, n)

        def carry_wait():
            nc.vector.sem_inc(carried, 1)

        def ln_load(b, t):
            if isinstance(b, int) and b == 0:
                return t // XRING + 1
            return 4 * b - 2 + t // XRING + 1

        def res_load(b, t):
            if isinstance(b, int) and b == B - 1:
                return 4 * b + 2 + t // XRING + 1
            return 4 * b + 4 + t // XRING + 1

        def stores(b, t):
            return 2 * b + t // XRING + 1

        def run(engine_loop, batch):
            batch(0, True, False)
            with engine_loop(1, B - 1) as b:
                batch(b, False, False)
            batch(B - 1, False, True)

        @block.sync
        def _(sp):
            def load_ln(b, t):
                r = t % XRING
                if t >= XRING:
                    sp.wait_ge(done["ht"], count(("ht", t - XRING), b - 1))
                elif not (isinstance(b, int) and b <= 1):
                    sp.wait_ge(out_stored[r], 16 * stores(b - 2, t + XRING))
                elif b == 1:
                    sp.wait_ge(done["ht"], count(("ht", t + XRING), -1))
                sp.dma_start(xt[:, r, :], x_tiles[b * TILES + t]).then_inc(x_loaded[r], 16)

            def load_res(b, t):
                r = t % XRING
                if t >= XRING or (isinstance(b, int) and b == B - 1):
                    before = stores(b, t - XRING) if t >= XRING else stores(b - 1, t + XRING)
                    sp.wait_ge(out_stored[r], 16 * before)
                else:
                    sp.wait_ge(done["ht"], count(("ht", t + XRING), b))
                sp.dma_start(xt[:, r, :], x_tiles[b * TILES + t]).then_inc(x_loaded[r], 16)

            def store(b, t):
                r = t % XRING
                sp.wait_ge(out_ready, b * TILES + t + 1)
                sp.dma_start(out_tiles[b * TILES + t], xt[:, r, :]).then_inc(out_stored[r], 16)

            def swap(unit, b):
                _, pair, i = unit
                a = pair % 2
                sp.wait_ge(read["qk"], count(unit, b))
                for side in range(2):
                    to = slice(side * HD, side * HD + HD)
                    fro = slice((1 - side) * HD, (1 - side) * HD + HD)
                    keys = slice(i * HALF, (i + 1) * HALF)
                    sp.dma_start(k_sw[to, a, :, keys], k_st[fro, a, :, keys]).then_inc(k_swapped[2 * i + side], 16)

            def batch(b, first, last):
                for s in range(SLOTS):
                    unit, of = ended(s, b, first, last)
                    if unit and unit[0] == "qk" and unit[2] < 2:
                        swap(unit, of)
                    for t in range(TILES):
                        if not first and s == PROJ_AT[t][-1] + 4:
                            store(b - 1, t)
                    for t in range(TILES):
                        if not first and s == max(0, PROJ_AT[t][0] - 4):
                            load_res(b - 1, t)
                        if not last and s == HT_AT[t][0] - 4:
                            load_ln(b + 1, t)

            for t in range(XRING):
                sp.dma_start(xt[:, t, :], x_tiles[t]).then_inc(x_loaded[t], 16)
            w_rows = w_qkv.rearrange("(k p) n -> k p n", p=P)
            for k in range(KT):
                sp.dma_start(w_stage[:, k, :], w_rows[k]).then_inc(w_loaded[k], 16)
            sp.dma_start(wo_stage, w_proj.rearrange("(k p) n -> p k n", p=P)).then_inc(w_out_loaded, 16)
            sp.dma_start(adj_stage, adj.rearrange("(t p) n -> p t n", p=P)).then_inc(adj_loaded, 16)
            for t in range(XRING, TILES):
                load_ln(0, t)
            for row, tile, signal in ((b_proj, bias_b, bias_loaded), (gamma, gamma_b, gamma_loaded),
                                      (beta, beta_b, beta_loaded)):
                sp.dma_start(tile[:], row.rearrange("(a n) -> a n", a=1).broadcast_to([P, D])).then_inc(signal, 16)
            for unit in PREPARE:
                if unit[0] == "qk" and unit[2] < 2:
                    swap(unit, -1)
            run(sp.Fori, batch)
            for t in range(TILES):
                load_res(B - 1, t)
                if t >= 1:
                    store(B - 1, t - 1)
            store(B - 1, TILES - 1)
            for r in range(XRING):
                sp.wait_ge(out_stored[r], 16 * stores(B - 1, XRING + r))

        @block.tensor
        def _(pe):
            def scores(b, w, s):
                g = b * SLOTS + w * STEPS + s
                a, h, j = w % 2, s % 2, 2 * (s // 4) + s % 4 // 2
                if s == 0:
                    pe.wait_ge(read["qk"], (b * PAIRS + w) * 4 + 3)
                    for i in range(4):
                        pe.wait_ge(k_swapped[i], 16 * (b * PAIRS + w + 1))
                if s == STEPS // 2:
                    pe.wait_ge(read["qk"], (b * PAIRS + w) * 4 + 4)
                since(pe, exp_ready, g - 1)
                for n in range(2):
                    keys = slice(n * HALF, (n + 1) * HALF)
                    q = q_st[:, a, h, j * P:(j + 1) * P]
                    nc.tensor.matmul(ps_s[:, s % 2, keys], q, k_sw[:, a, h, keys], start=True, stop=False)
                    last = nc.tensor.matmul(ps_s[:, s % 2, keys], q, k_st[:, a, h, keys], start=False, stop=True)
                last.then_inc(scores_ready, 1)

            def transposes(g, parity):
                pe.wait_ge(probs_ready, g + 1)
                for half in range(2):
                    since(pe, pt_ready, 2 * g - 1 + half)
                    for i in range(4):
                        t = half * 4 + i
                        last = nc.tensor.transpose(ps_t[:, half, i, :], probs[:, parity, t * P:(t + 1) * P], ident[:])
                    last.then_inc(transposed, 1)

            def values(b, w, c, part):
                n = (b * PAIRS + w) * CHUNKS + c
                if part == 0:
                    pe.wait_ge(pt_ready, 8 * (n + 1))
                    since(pe, ot_ready, n)
                    if c == 0 and w % 2 == 0:
                        pe.wait_ge(read["v"], (b * 2 + w // 2 + 1) * 4)
                for t in (2 * part, 2 * part + 1):
                    for h in range(2):
                        col = (w % 2) * P + h * HD
                        last = nc.tensor.matmul(ps_o[h * HD:(h + 1) * HD, :], v[:, w // 2, t, col:col + HD],
                                                pt[:, c % 2, h, t, :], start=(t == 0), stop=(t == TILES - 1))
                if part == 3:
                    last.then_inc(heads_ready, 1)

            def split_matmuls(dst, stationary, moving, tiles):
                for k in tiles:
                    for sa, mo in ((0, 1), (1, 0), (0, 0)):
                        last = nc.tensor.matmul(dst, stationary(k, sa), moving(k, mo), start=(k == 0 and mo == 1),
                                                stop=(k == KT - 1 and sa == mo))
                return last

            def do(unit, part, parts, b, before, bank):
                if before and part == 0:
                    pe.wait_ge(read[before[0][0]], count(*before))
                kind = unit[0]
                w_, wo_, h_, o_ = (w_hi, w_lo), (wo_hi, wo_lo), (ht_hi, ht_lo), (ot_hi, ot_lo)
                if kind in ("qk", "v") and part == 0:
                    there = (b + 1 if for_next(unit) else b) * TILES
                    pe.wait_ge(read["ht"], there + (4 * (unit[2] % 2) + 4 if kind == "qk" else 2 * unit[2] + 2))
                tiles = range(part * KT // parts, (part + 1) * KT // parts)
                if kind == "proj":
                    t = unit[1]
                    if part == 0:
                        pe.wait_ge(ot_ready, ((b - 1) * PAIRS + PAIRS - 1) * CHUNKS + t // 2 + 1)
                    last = split_matmuls(bank, lambda k, e: o_[e][:, k, t * P:(t + 1) * P],
                                         lambda k, e: wo_[e][:, k, :], tiles)
                elif kind == "ht":
                    t = unit[1]
                    pe.wait_ge(h_ready, count(unit, b))
                    for k in range(KT):
                        last = nc.tensor.transpose(bank[:, k * P:(k + 1) * P],
                                                   xt[:, t % XRING, k * P:(k + 1) * P], ident[:])
                elif kind == "qk":
                    _, pair, i = unit
                    col = (D if i < 2 else 0) + pair * P
                    rows = slice(i % 2 * HALF, (i % 2 + 1) * HALF)
                    last = split_matmuls(bank, lambda k, e: w_[e][:, k, col:col + P],
                                         lambda k, e: h_[e][:, k, rows], tiles)
                else:
                    _, half, i = unit
                    col = 2 * D + half * 2 * P
                    for e2 in range(2 * part // parts, 2 * (part + 1) // parts):
                        rows = slice((2 * i + e2) * P, (2 * i + e2 + 1) * P)
                        last = split_matmuls(bank[:, e2 * 2 * P:(e2 + 1) * 2 * P],
                                             lambda k, e: h_[e][:, k, rows],
                                             lambda k, e: w_[e][:, k, col:col + 2 * P], range(KT))
                if part == parts - 1:
                    last.then_inc(done[kind], 1)

            def batch(b, first, last):
                before = (PREPARE[-1], b - 1)
                for s in range(SLOTS):
                    g = b * SLOTS + s
                    scores(b, s // STEPS, s % STEPS)
                    if s >= 2 or not first:
                        transposes(g - 2, s % 2)
                    c, part = divmod(s - 6, 4)
                    if c >= 0:
                        values(b, c // CHUNKS, c % CHUNKS, part)
                    elif not first:
                        values(b - 1, PAIRS - 1, CHUNKS + c, part)
                    unit, part, parts = FILL[s]
                    if has(unit, first, last):
                        do(unit, part, parts, b, before, ps_f[:])
                        if part == parts - 1:
                            before = (unit, b)

            pe.wait_ge(ident_ready, 1)
            for n, unit in enumerate(PREPARE):
                if unit == next(u for u in PREPARE if u[0] != "ht"):
                    pe.wait_ge(w_ready, KT)
                before = (PREPARE[n - len(spare)], -1) if n >= len(spare) else None
                do(unit, 0, 1, -1, before, spare[n % len(spare)])
            pe.wait_ge(read["v"], 4)
            pe.wait_ge(w_ready, KT + 1)
            run(pe.Fori, batch)
            for g in range(B * SLOTS - 2, B * SLOTS):
                transposes(g, g % 2)
            for part in (2, 3):
                values(B - 1, PAIRS - 1, CHUNKS - 2, part)
            for part in range(4):
                values(B - 1, PAIRS - 1, CHUNKS - 1, part)
            for t in range(TILES):
                n = t - len(spare)
                before = (("proj", n), B) if n >= 0 else None
                do(("proj", t), 0, 1, B, before, spare[t % len(spare)])

        @block.vector
        def _(dve):
            def normalise(g, parity):
                dve.wait_ge(exp_ready, g + 1)
                nc.vector.reciprocal(inv_sum[:, parity:parity + 1], row_sum[:, parity:parity + 1]).then_inc(inverted, 1)
                dve.wait_ge(inverted, g + 1)
                nc.vector.tensor_scalar(probs[:, parity, :], probs[:, parity, :], inv_sum[:, parity:parity + 1],
                                        None, ALU.mult).then_inc(probs_ready, 1)

            def mask_and_max(g, s):
                dve.wait_ge(scores_ready, g + 1)
                carry_wait()
                j = 2 * (s // 4) + s % 4 // 2
                nc.vector.tensor_tensor_reduce(ps_s[:, s % 2, :], ps_s[:, s % 2, :], mask[:, j, :], score_scale[:],
                                               HUGE, ALU.add, ALU.min, neg_max[:, s % 2:s % 2 + 1]).then_inc(masked, 1)

            def low_heads(b, w, c):
                n = (b * PAIRS + w) * CHUNKS + c + 1
                dve.wait_ge(ot_high, n)
                rows = slice(c * 2 * P, (c + 1) * 2 * P)
                nc.vector.tensor_tensor(ot_lo[:, w, rows], ps_o[:], ot_hi[:, w, rows], ALU.subtract).then_inc(ot_ready, 1)

            def take(unit, b, bank):
                kind, n = unit[0], count(unit, b)
                dve.wait_ge(done[kind], n)
                if kind == "proj":
                    t = unit[1]
                    dve.wait_ge(x_plus_o, n)
                    nc.vector.scalar_tensor_tensor(
                        out=o_t[:, t % 2, :], in0=bank, scalar=proj_scale[:].bitcast(F32), in1=bias_b[:],
                        op0=ALU.mult, op1=ALU.add).then_inc(read[kind], 1)
                elif kind == "ht":
                    rows = slice(unit[1] * P, (unit[1] + 1) * P)
                    dve.wait_ge(high[kind], n)
                    nc.vector.scalar_tensor_tensor(
                        out=ht_lo[:, :, rows], in0=bank.rearrange("p (k n) -> p k n", k=KT),
                        scalar=2.0 ** H_SCALE_LOG2, in1=ht_hi[:, :, rows], op0=ALU.mult,
                        op1=ALU.subtract).then_inc(read[kind], 1)
                elif kind == "qk":
                    _, pair, i = unit
                    dst = k_st if i < 2 else q_st
                    rows = slice(i % 2 * HALF, (i % 2 + 1) * HALF)
                    dve.wait_ge(high[kind], n)
                    for h in range(2):
                        here = slice(h * HD, (h + 1) * HD)
                        there = slice((1 - h) * HD, (1 - h) * HD + HD)
                        last = nc.vector.scalar_tensor_tensor(
                            out=dst[there, pair % 2, h, rows], in0=bank[here, :], scalar=OUT_OF_PSUM,
                            in1=dst[here, pair % 2, h, rows], op0=ALU.mult, op1=ALU.subtract)
                    last.then_inc(read[kind], 1)
                else:
                    _, half, i = unit
                    nc.vector.tensor_scalar(v[:, half, 2 * i:2 * i + 2, :], bank.rearrange("p (e n) -> p e n", e=2),
                                            OUT_OF_PSUM, None, ALU.mult).then_inc(read[kind], 1)

            def o_statistics(t, n):
                dve.wait_ge(read["proj"], n)
                nc.vector.bn_stats(o_st[:, t % 2, :], o_t[:, t % 2, :]).then_inc(o_stats, 1)
                dve.wait_ge(o_stats, n)
                carry_wait()
                nc.vector.bn_aggr(o_mv[:, t % 2, :], o_st[:, t % 2, :]).then_inc(o_moments, 1)

            def standardise(b, t):
                n = b * TILES + t + 1
                dve.wait_ge(o_dev, n)
                since(dve, out_ready, n - 1)
                nc.vector.tensor_scalar(norm_t[:], o_t[:, t % 2, :], o_mv[:, t % 2, 0:1], o_aff[:, t % 2, 1:2],
                                        ALU.subtract, ALU.mult).then_inc(o_normed, 1)

            def x_statistics(b, t):
                n = b * TILES + t + 1
                dve.wait_ge(x_loaded[t % XRING], 16 * ln_load(b, t))
                since(dve, x_affine, n - 2)
                nc.vector.bn_stats(x_st[:, t % 2, :], xt[:, t % XRING, :]).then_inc(x_stats, 1)
                dve.wait_ge(x_stats, n)
                carry_wait()
                nc.vector.bn_aggr(x_mv[:, t % 2, :], x_st[:, t % 2, :]).then_inc(x_moments, 1)

            def batch(b, first, last):
                for s in range(SLOTS):
                    g = b * SLOTS + s
                    unit, of = ended(s, b, first, last)
                    if s % 4 == 2:
                        c = (s - 10) // 4
                        if c >= 0:
                            low_heads(b, c // CHUNKS, c % CHUNKS)
                        elif not first:
                            low_heads(b - 1, PAIRS - 1, CHUNKS + c)
                    if unit:
                        take(unit, of, ps_f[:])
                    mask_and_max(g, s % STEPS)
                    if s > 0 or not first:
                        normalise(g - 1, (s - 1) % 2)
                    if unit and unit[0] == "proj":
                        o_statistics(unit[1], count(unit, of))
                    for t in range(TILES):
                        if not first and s == PROJ_AT[t][-1] + 2:
                            standardise(b - 1, t)
                        if not last and s == HT_AT[t][0] - 2:
                            x_statistics(b + 1, t)

            steps = [0]

            def prep(instruction):
                instruction.then_inc(w_prep, 1)
                steps[0] += 1
                dve.wait_ge(w_prep, steps[0])

            def largest(matrix, tiles):
                for k, (tile, dst) in enumerate(tiles):
                    dve.wait_ge(w_out_loaded if matrix else w_loaded[k], 16)
                    size = tile.shape[-1]
                    prep(nc.vector.tensor_scalar(w_abs[:, 0:size], tile.bitcast(I32), 0x7FFFFFFF, None,
                                                 ALU.bitwise_and))
                    prep(nc.vector.tensor_reduce(dst, w_abs[:, 0:size].bitcast(F32), AX_X, ALU.max))

            def scale(matrix):
                a = slice(matrix, matrix + 1)
                dve.wait_ge(w_max_ready, matrix + 1)
                prep(nc.vector.tensor_scalar(top_bits[:, a], w_all[:, a].bitcast(I32), 0x7F800000, None,
                                             ALU.bitwise_and))
                prep(nc.vector.tensor_scalar(clamped_bits[:, a], top_bits[:, a], float(80 << MANT), None, ALU.max))
                nc.vector.tensor_scalar(w_scale[:, a], clamped_bits[:, a], -1.0, float((254 + W_TOP_LOG2) << MANT),
                                        ALU.mult, ALU.add).then_inc(scale_ready, 1)
                dve.wait_ge(scale_ready, matrix + 1)

            for t in range(2):
                x_statistics(0, t)
            largest(0, [(w_stage[:, k, :], w_part[:, k:k + 1]) for k in range(KT)])
            prep(nc.vector.tensor_reduce(w_top[:, 0:1], w_part[:], AX_X, ALU.max))
            nc.vector.sem_inc(w_top_ready, 1)
            scale(0)
            for k in range(KT):
                dve.wait_ge(w_high, k + 1)
                nc.vector.scalar_tensor_tensor(out=w_lo[:, k, :], in0=w_stage[:, k, :],
                                               scalar=w_scale[:, 0:1].bitcast(F32), in1=w_hi[:, k, :],
                                               op0=ALU.mult, op1=ALU.subtract).then_inc(w_ready, 1)
            prep(nc.vector.tensor_scalar(
                product_bits[:, 0:1], clamped_bits[:, 0:1], 2.0,
                -float((127 + 2 * (W_TOP_LOG2 + ATT_LOG2) + ATT_LOG2_SCALE) << MANT), ALU.mult, ALU.add))
            prep(nc.vector.tensor_scalar(score_scale[:], product_bits[:, 0:1].bitcast(F32), -1.0, None, ALU.mult))
            for n, unit in enumerate(PREPARE):
                if unit[0] == "ht" and unit[1] + 2 < TILES:
                    x_statistics(0, unit[1] + 2)
                take(unit, -1, spare[n % len(spare)])
                if n == TILES + 1:
                    largest(1, [(wo_stage.rearrange("p k n -> p (k n)"), w_top[:, 1:2])])
                    nc.vector.sem_inc(w_top_ready, 1)
                if n == TILES + 3:
                    dve.wait_ge(adj_loaded, 16)
                    nc.vector.tensor_scalar(mask[:], adj_stage, 0.0, MASKED, ALU.is_equal,
                                            ALU.mult).then_inc(mask_ready, 1)
            scale(1)
            dve.wait_ge(w_high, KT + 1)
            nc.vector.scalar_tensor_tensor(
                out=wo_lo[:].rearrange("p k n -> p (k n)"), in0=wo_stage.rearrange("p k n -> p (k n)"),
                scalar=w_scale[:, 1:2].bitcast(F32), in1=wo_hi[:].rearrange("p k n -> p (k n)"),
                op0=ALU.mult, op1=ALU.subtract).then_inc(w_ready, 1)
            prep(nc.vector.tensor_scalar(product_bits[:, 1:2], clamped_bits[:, 0:1],
                                         -float((127 + 2 * W_TOP_LOG2 + ATT_LOG2) << MANT), None, ALU.add))
            prep(nc.vector.tensor_tensor(proj_scale[:], product_bits[:, 1:2], clamped_bits[:, 1:2], ALU.add))
            dve.wait_ge(mask_ready, 1)
            dve.wait_ge(bias_loaded, 16)
            run(dve.Fori, batch)
            normalise(B * SLOTS - 1, 1)
            for c in (CHUNKS - 2, CHUNKS - 1):
                low_heads(B - 1, PAIRS - 1, c)
            for t in range(TILES + 1):
                if t < TILES:
                    if t >= 2:
                        dve.wait_ge(o_normed, (B - 1) * TILES + t - 1)
                    take(("proj", t), B, spare[t % len(spare)])
                    o_statistics(t, count(("proj", t), B))
                if t:
                    standardise(B - 1, t - 1)

        @block.scalar
        def _(act):
            def high_part(unit, b, bank):
                kind, n = unit[0], count(unit, b)
                act.wait_ge(done[kind], n)
                if kind == "ht":
                    rows = slice(unit[1] * P, (unit[1] + 1) * P)
                    nc.scalar.activation(ht_hi[:, :, rows], bank.rearrange("p (k n) -> p k n", k=KT),
                                         ACT.Copy, scale=2.0 ** H_SCALE_LOG2).then_inc(high[kind], 1)
                else:
                    _, pair, i = unit
                    dst = k_st if i < 2 else q_st
                    rows = slice(i % 2 * HALF, (i % 2 + 1) * HALF)
                    for h in range(2):
                        here = slice(h * HD, (h + 1) * HD)
                        last = nc.scalar.activation(dst[here, pair % 2, h, rows], bank[here, :], ACT.Copy,
                                                    scale=OUT_OF_PSUM)
                    last.then_inc(high[kind], 1)

            def copy_transposed(g, s, n):
                if s % 4 == 0:
                    since(act, heads_ready, n - 1)
                h, c, col = s % 2, s // 4 % 2, s % 4 // 2 * P
                for half in range(2):
                    act.wait_ge(transposed, 2 * g + half + 1)
                    nc.scalar.activation(pt[:, c, h, half * 4:half * 4 + 4, col:col + P], ps_t[:, half, :, :],
                                         ACT.Copy).then_inc(pt_ready, 1)

            def copy_heads(b, w, c):
                act.wait_ge(heads_ready, (b * PAIRS + w) * CHUNKS + c + 1)
                nc.scalar.activation(ot_hi[:, w, c * 2 * P:(c + 1) * 2 * P], ps_o[:],
                                     ACT.Copy).then_inc(ot_high, 1)

            def exponential(g, parity):
                act.wait_ge(masked, g + 1)
                since(act, transposed, 2 * (g - 1))
                nc.scalar.activation(probs[:, parity, :], ps_s[:, parity, :], ACT.Exp,
                                     bias=neg_max[:, parity:parity + 1], scale=-1.0,
                                     accum_out=row_sum[:, parity:parity + 1]).then_inc(exp_ready, 1)

            def relu_norm(b, t):
                act.wait_ge(x_affine, b * TILES + t + 1)
                nc.scalar.activation(xt[:, t % XRING, :], xt[:, t % XRING, :], ACT.Relu,
                                     bias=x_aff[:, t % 2, 3:4], scale=x_aff[:, t % 2, 1:2]).then_inc(h_ready, 1)

            def batch(b, first, last):
                for s in range(SLOTS):
                    g = b * SLOTS + s
                    if s % 4 == 2:
                        c = (s - 10) // 4
                        if c >= 0:
                            copy_heads(b, c // CHUNKS, c % CHUNKS)
                        elif not first:
                            copy_heads(b - 1, PAIRS - 1, CHUNKS + c)
                    unit, of = ended(s, b, first, last)
                    if unit and unit[0] in ("ht", "qk"):
                        high_part(unit, of, ps_f[:])
                    if s >= 2 or not first:
                        copy_transposed(g - 2, (s - 2) % STEPS, b * (SLOTS // 4) + (s - 2) // 4)
                    exponential(g, s % 2)
                    for t in range(TILES):
                        if not last and s == HT_AT[t][0] - 1:
                            relu_norm(b + 1, t)

            relu_norm(0, 0)
            act.wait_ge(scale_ready, 1)
            for k in range(KT):
                nc.scalar.activation(w_hi[:, k, :], w_stage[:, k, :], ACT.Copy,
                                     scale=w_scale[:, 0:1].bitcast(F32)).then_inc(w_high, 1)
            for n, unit in enumerate(PREPARE):
                if unit[0] == "ht" and unit[1] + 1 < TILES:
                    relu_norm(0, unit[1] + 1)
                if unit[0] != "v":
                    high_part(unit, -1, spare[n % len(spare)])
            act.wait_ge(scale_ready, 2)
            nc.scalar.activation(wo_hi[:], wo_stage, ACT.Copy, scale=w_scale[:, 1:2].bitcast(F32)).then_inc(w_high, 1)
            run(act.Fori, batch)
            for g in range(B * SLOTS - 2, B * SLOTS):
                copy_transposed(g, g % STEPS, g // 4)
            for c in (CHUNKS - 2, CHUNKS - 1):
                copy_heads(B - 1, PAIRS - 1, c)

        @block.gpsimd
        def _(pool):
            def x_scale_and_shift(b, t):
                n, a = b * TILES + t + 1, t % 2
                pool.wait_ge(x_moments, n)
                since(pool, h_ready, n - 2)
                nc.gpsimd.tensor_tensor(x_aff[:, a, 0:1], x_mv[:, a, 1:2], eps[:], ALU.add).then_inc(x_var, 1)
                nc.gpsimd.tensor_tensor(x_aff[:, a, 2:3], x_mv[:, a, 0:1], minus_one[:], ALU.mult).then_inc(x_neg, 1)
                pool.wait_ge(x_var, n)
                nc.gpsimd.tensor_tensor(x_aff[:, a, 1:2], x_aff[:, a, 0:1], minus_half[:], ALU.pow).then_inc(x_dev, 1)
                pool.wait_ge(x_neg, n)
                pool.wait_ge(x_dev, n)
                nc.gpsimd.tensor_tensor(x_aff[:, a, 3:4], x_aff[:, a, 2:3], x_aff[:, a, 1:2],
                                        ALU.mult).then_inc(x_affine, 1)

            def add_beta(b, t):
                n, r = b * TILES + t + 1, t % XRING
                pool.wait_ge(x_loaded[r], 16 * res_load(b, t))
                nc.gpsimd.tensor_tensor(xt[:, r, :], xt[:, r, :], beta_b[:], ALU.add).then_inc(x_plus_beta, 1)

            def finish(b, t):
                n, r, a = b * TILES + t + 1, t % XRING, t % 2
                pool.wait_ge(o_moments, n)
                nc.gpsimd.tensor_tensor(o_aff[:, a, 0:1], o_mv[:, a, 1:2], eps[:], ALU.add).then_inc(o_var, 1)
                pool.wait_ge(o_var, n)
                nc.gpsimd.tensor_tensor(o_aff[:, a, 1:2], o_aff[:, a, 0:1], minus_half[:], ALU.pow).then_inc(o_dev, 1)
                pool.wait_ge(x_plus_beta, n)
                nc.gpsimd.tensor_tensor(xt[:, r, :], xt[:, r, :], o_t[:, a, :], ALU.add).then_inc(x_plus_o, 1)
                pool.wait_ge(o_normed, n)
                nc.gpsimd.tensor_tensor(norm_t[:], norm_t[:], gamma_b[:], ALU.mult).then_inc(o_gamma, 1)
                pool.wait_ge(o_gamma, n)
                pool.wait_ge(x_plus_o, n + 2)
                nc.gpsimd.tensor_tensor(xt[:, r, :], xt[:, r, :], norm_t[:], ALU.add).then_inc(out_ready, 1)

            def batch(b, first, last):
                if not first:
                    add_beta(b - 1, 0)
                    for t in range(TILES):
                        if t + 1 < TILES:
                            add_beta(b - 1, t + 1)
                        finish(b - 1, t)
                if not last:
                    for t in range(TILES):
                        x_scale_and_shift(b + 1, t)

            nc.gpsimd.memset(ident[:], 0.0).then_inc(zeroed, 1)
            for tile, value in ((minus_half, -0.5), (minus_one, -1.0), (eps, EPS)):
                nc.gpsimd.memset(tile[:], value).then_inc(consts_ready, 1)
            for a in range(2):
                nc.gpsimd.memset(o_t[:, a, :], 0.0).then_inc(x_plus_o, 1)
            pool.wait_ge(zeroed, 1)
            nc.gpsimd.affine_select(out=ident[:], in_=ident[:], compare_op=ALU.not_equal, fill=1.0, base=0,
                                    pattern=[[-1, P]], channel_multiplier=1).then_inc(ident_ready, 1)
            pool.wait_ge(consts_ready, 3)
            x_scale_and_shift(0, 0)
            x_scale_and_shift(0, 1)
            pool.wait_ge(w_top_ready, 1)
            nc.gpsimd.partition_all_reduce(w_all[:, 0:1], w_top[:, 0:1], P, RMAX).then_inc(w_max_ready, 1)
            for t in range(2, TILES):
                x_scale_and_shift(0, t)
            pool.wait_ge(w_top_ready, 2)
            nc.gpsimd.partition_all_reduce(w_all[:, 1:2], w_top[:, 1:2], P, RMAX).then_inc(w_max_ready, 1)
            pool.wait_ge(beta_loaded, 16)
            pool.wait_ge(gamma_loaded, 16)
            run(pool.Fori, batch)
            add_beta(B - 1, 0)
            for t in range(TILES):
                if t + 1 < TILES:
                    add_beta(B - 1, t + 1)
                finish(B - 1, t)


INPUTS = ("x", "adj", "L0_gnn_w_qkv", "L0_gnn_w_proj", "L0_gnn_b_proj", "L0_gnn_ln_gamma", "L0_gnn_ln_beta")


def kernel(**inputs):
    import concourse.bacc as bacc
    from concourse.bass_utils import run_bass_kernel_spmd

    nc = bacc.Bacc("TRN2", target_bir_lowering=False, num_devices=1)
    arrays, args = {}, []
    for name in INPUTS:
        a = np.ascontiguousarray(inputs[name])
        arrays[f"in_{name}"] = a
        args.append(nc.dram_tensor(f"in_{name}", a.shape, mybir.dt.from_np(a.dtype), kind="ExternalInput").ap())
    args.append(nc.dram_tensor("out", (B, N, D), F32, kind="ExternalOutput").ap())
    build(nc, *args)
    r = run_bass_kernel_spmd(nc, [arrays], core_ids=[0])
    return r.results[0]["out"]
```

```python
from contextlib import ExitStack

import numpy as np

import concourse.bass as bass
from concourse import mybir

P = 128
B, N, D = 16, 1024, 512
HEADS = 8
HD = D // HEADS
TILES = N // P
KT = D // P
PAIRS = HEADS // 2
STEPS = 2 * TILES
CHUNKS = TILES // 2
SLOTS = PAIRS * STEPS
HALF = N // 2
RING = 4

F32 = mybir.dt.float32
F16 = mybir.dt.float16
BF16 = mybir.dt.bfloat16
I32 = mybir.dt.int32
ALU = mybir.AluOpType
ACT = mybir.ActivationFunctionType
AX_X = mybir.AxisListType.X
RMAX = bass.bass_isa.ReduceOp.max

EPS = 1e-5
ATT_LOG2_SCALE = 3
assert 4**ATT_LOG2_SCALE == HD
MASKED = -(2.0 ** 126)
HUGE = 3e38
H_SCALE_LOG2 = 8
W_TOP_LOG2 = 13
ATT_LOG2 = -8
OUT_OF_PSUM = 2.0 ** (ATT_LOG2 - H_SCALE_LOG2)
MANT = 23


PROJ_AT = ((0, 1), (2, 3), (5, 6), (7, 8), (12, 13), (14, 15), (16, 17), (18, 19))
HT_AT = ((41,), (42,), (43,), (44,), (46,), (47,), (49,), (50,))
STATS_AT = tuple(22 + 2 * t for t in range(TILES))
QK_AT = (((51, 52), (53, 54), (57, 58), (61, 62, 63)), ((4,), (9,), (10, 11), (20, 21)),
         ((22, 23), (24, 25), (26, 27), (32, 33)), ((35,), (36, 37), (38,), (39,)))
V_AT = (((45,), (48,), (55, 56), (59, 60)), ((28, 29), (30, 31), (34,), (40,)))

UNITS = {("proj", t): slots for t, slots in enumerate(PROJ_AT)}
UNITS |= {("ht", t): slots for t, slots in enumerate(HT_AT)}
UNITS |= {("qk", n, i): slots for n, at in enumerate(QK_AT) for i, slots in enumerate(at)}
UNITS |= {("v", n, i): slots for n, at in enumerate(V_AT) for i, slots in enumerate(at)}
FILL = {s: (unit, i, len(slots)) for unit, slots in UNITS.items() for i, s in enumerate(slots)}
assert len(FILL) == SLOTS == sum(len(slots) for slots in UNITS.values())
ENDS = {slots[-1]: unit for unit, slots in UNITS.items()}

EARLY = {s for slots in HT_AT for s in slots}


def for_next(unit):
    return unit[0] == "ht" or unit[0] in ("qk", "v") and unit[1] == 0


START = {0: ("qk", 0, 3), 1: ("v", 0, 0), 2: ("v", 0, 1), 3: ("v", 0, 2), 5: ("v", 0, 3)}
assert all(FILL[s][0][0] == "proj" for s in START)


def build(nc, x, adj, w_qkv, w_proj, b_proj, gamma, beta, out):
    x_tiles = x.rearrange("b (t p) d -> (b t) p d", p=P)
    out_tiles = out.rearrange("b (t p) d -> (b t) p d", p=P)

    with ExitStack() as ctx:
        def sb(name, shape, dt):
            return ctx.enter_context(nc.sbuf_tensor(name, shape, dt))

        def psum(name, shape, dt):
            return ctx.enter_context(nc.psum_tensor(name, shape, dt))

        def sem(name):
            return ctx.enter_context(nc.semaphore(name))

        mask = sb("mask", [P, TILES, N], BF16)
        w_hi = sb("w_hi", [P, KT, 3 * D], F16)
        w_lo = sb("w_lo", [P, KT, 3 * D], F16)
        wo_hi = sb("wo_hi", [P, KT, D], F16)
        wo_lo = sb("wo_lo", [P, KT, D], F16)
        bias_b = sb("bias_b", [P, D], F32)
        gamma_b = sb("gamma_b", [P, D], F32)
        beta_b = sb("beta_b", [P, D], F32)
        ident = sb("ident", [P, P], F32)
        ht_hi = sb("ht_hi", [P, KT, N], F16)
        ht_lo = sb("ht_lo", [P, KT, N], F16)
        q_st = sb("q_st", [P, 2, 2, N], F16)
        k_st = sb("k_st", [P, 2, 2, N], F16)
        k_sw = sb("k_sw", [P, 2, 2, N], F16)
        v = sb("v", [P, 2, TILES, 2 * P], F32)
        probs = sb("probs", [P, 2, N], F32)
        pt = sb("pt", [P, 2, 2, TILES, 2 * P], F32)
        ot_hi = sb("ot_hi", [P, PAIRS, N], F16)
        ot_lo = sb("ot_lo", [P, PAIRS, N], F16)
        xt = sb("xt", [P, RING, D], F32)
        o_t = sb("o_t", [P, 2, D], F32)
        norm_t = sb("norm_t", [P, D], F32)
        neg_max = sb("neg_max", [P, 2], F32)
        row_sum = sb("row_sum", [P, 2], F32)
        inv_sum = sb("inv_sum", [P, 2], F32)
        x_st = sb("x_st", [P, 2, 6], F32)
        x_mv = sb("x_mv", [P, 2, 2], F32)
        x_aff = sb("x_aff", [P, 2, 4], F32)
        o_st = sb("o_st", [P, 2, 6], F32)
        o_mv = sb("o_mv", [P, 2, 2], F32)
        o_aff = sb("o_aff", [P, 2, 2], F32)
        minus_half = sb("minus_half", [P, 1], F32)
        minus_one = sb("minus_one", [P, 1], F32)
        eps = sb("eps", [P, 1], F32)
        w_stage = sb("w_stage", [P, KT, 3 * D], F32)
        x_next = w_stage[:].rearrange("p k n -> p (k n)")[:, 0:TILES * D].rearrange("p (t n) -> p t n", t=TILES)
        wo_stage = v[:, 1].rearrange("p t n -> p (t n)").rearrange("p (k n) -> p k n", k=KT)
        w_abs = ot_lo[:].rearrange("p a n -> p (a n)").bitcast(I32)
        w_qkv_abs = [tile[:].rearrange(axes).bitcast(F32)[:, 0:3 * D] for tile, axes in (
            (q_st, "p a h n -> p (a h n)"), (k_st, "p a h n -> p (a h n)"), (k_sw, "p a h n -> p (a h n)"),
            (ot_hi, "p a n -> p (a n)"))]
        w_part = sb("w_part", [P, KT], F32)
        w_top = sb("w_top", [P, 2], F32)
        w_all = sb("w_all", [P, 2], F32)
        top_bits = sb("top_bits", [P, 2], I32)
        clamped_bits = sb("clamped_bits", [P, 2], I32)
        w_scale = sb("w_scale", [P, 2], I32)
        product_bits = sb("product_bits", [P, 2], I32)
        score_scale = sb("score_scale", [P, 1], F32)
        proj_scale = sb("proj_scale", [P, 1], I32)
        adj_stage = pt[:].rearrange("p a h t n -> p (a h t n)").rearrange("p (t n) -> p t n", t=TILES)

        ps_s = psum("ps_s", [P, 2, N], F32)
        ps_t = psum("ps_t", [P, 2, 4, P], F32)
        ps_o = psum("ps_o", [P, 2 * P], F32)
        ps_f = psum("ps_f", [P, HALF], F32)

        spare = [ps_f[:], *(ps_t[:, half].rearrange("p a n -> p (a n)") for half in range(2))]
        spare_qk = [ps_s[:, 1, 0:HALF], ps_s[:, 1, HALF:N], ps_s[:, 0, HALF:N]]

        x_loaded = [sem(f"x_loaded{r}") for r in range(RING)]
        out_stored = [sem(f"out_stored{r}") for r in range(RING)]
        k_swapped = [sem(f"k_swapped{i}") for i in range(4)]
        w_loaded = [sem(f"w_loaded{k}") for k in range(KT)]
        adj_loaded = [sem(f"adj_loaded{half}") for half in range(2)]
        x_next_loaded = [sem(f"x_next_loaded{half}") for half in range(2)]
        w_out_loaded = sem("w_out_loaded")
        bias_loaded = sem("bias_loaded")
        gamma_loaded = sem("gamma_loaded")
        beta_loaded = sem("beta_loaded")
        zeroed = sem("zeroed")
        ident_ready = sem("ident_ready")
        consts_ready = sem("consts_ready")
        w_sized = sem("w_sized")
        w_prep = sem("w_prep")
        w_top_ready = sem("w_top_ready")
        w_max_ready = sem("w_max_ready")
        scale_ready = sem("scale_ready")
        w_high = sem("w_high")
        w_ready = sem("w_ready")
        mask_ready = sem("mask_ready")
        scores_ready = sem("scores_ready")
        masked = sem("masked")
        exp_ready = sem("exp_ready")
        inverted = sem("inverted")
        probs_ready = sem("probs_ready")
        transposed = sem("transposed")
        pt_ready = sem("pt_ready")
        heads_ready = sem("heads_ready")
        ot_high = sem("ot_high")
        ot_ready = sem("ot_ready")
        done = {k: sem(f"{k}_done") for k in ("ht", "qk", "v", "proj")}
        high = {k: sem(f"{k}_high") for k in ("ht", "qk")}
        read = {k: sem(f"{k}_read") for k in ("ht", "qk", "v", "proj")}
        x_stats = sem("x_stats")
        x_moments = sem("x_moments")
        x_var = sem("x_var")
        x_neg = sem("x_neg")
        x_dev = sem("x_dev")
        x_affine = sem("x_affine")
        h_ready = sem("h_ready")
        o_stats = sem("o_stats")
        o_moments = sem("o_moments")
        o_var = sem("o_var")
        o_dev = sem("o_dev")
        o_normed = sem("o_normed")
        x_plus_beta = sem("x_plus_beta")
        x_plus_o = sem("x_plus_o")
        o_gamma = sem("o_gamma")
        out_ready = sem("out_ready")
        carried = sem("carried")

        block = ctx.enter_context(nc.Block())

        def count(unit, b):
            if unit[0] == "proj":
                return (b - 1) * TILES + unit[1] + 1
            if unit[0] == "ht":
                return (b + 1) * TILES + unit[1] + 1
            ahead = 1 if unit[1] == 0 else 0
            if unit[0] == "qk":
                return ((b + ahead) * PAIRS + unit[1]) * 4 + unit[2] + 1
            return ((b + ahead) * 2 + unit[1]) * 4 + unit[2] + 1

        def has(unit, first, last):
            return not (first and unit[0] == "proj") and not (last and for_next(unit))

        def ended(s, b, first, last):
            if s == 0:
                return (None, b) if first else (ENDS.get(SLOTS - 1), b - 1)
            if first and s - 1 in START:
                return START[s - 1], -1
            if s - 1 in EARLY:
                return None, b
            unit = ENDS.get(s - 1)
            return (unit if unit and has(unit, first, last) else None), b

        def since(eng, signal, n):
            if isinstance(n, int) and n <= 0:
                return
            eng.wait_ge(signal, n)

        def carry_wait():
            nc.vector.sem_inc(carried, 1)

        def ln_tile(t, first):
            return xt[:, t % RING, :] if first else x_next[:, t, :]

        def res_load(b, t):
            return 2 * (b + 1) + t // RING + 1

        def stores(b, t):
            return 2 * b + t // RING + 1

        def run(engine_loop, batch):
            batch(0, True, False)
            with engine_loop(1, B - 1) as b:
                batch(b, False, False)
            batch(B - 1, False, True)

        @block.sync
        def _(sp):
            def load_x_next(b, half):
                tiles = slice(half * TILES // 2, (half + 1) * TILES // 2)
                x_rows = x[b].rearrange("(t p) d -> p t d", p=P)
                sp.dma_start(x_next[:, tiles, :], x_rows[:, tiles, :]).then_inc(x_next_loaded[half], 16)

            def load_res(b, t):
                r = t % RING
                if t >= RING:
                    sp.wait_ge(out_stored[r], 16 * stores(b, t - RING))
                elif isinstance(b, int) and b == 0:
                    sp.wait_ge(done["ht"], count(("ht", t + RING), -1))
                else:
                    sp.wait_ge(out_stored[r], 16 * stores(b - 1, t + RING))
                sp.dma_start(xt[:, r, :], x_tiles[b * TILES + t]).then_inc(x_loaded[r], 16)

            def store(b, t):
                r = t % RING
                sp.wait_ge(out_ready, b * TILES + t + 1)
                sp.dma_start(out_tiles[b * TILES + t], xt[:, r, :]).then_inc(out_stored[r], 16)

            def swap(unit, b):
                _, pair, i = unit
                a = pair % 2
                sp.wait_ge(read["qk"], count(unit, b))
                for side in range(2):
                    to = slice(side * HD, side * HD + HD)
                    fro = slice((1 - side) * HD, (1 - side) * HD + HD)
                    keys = slice(i * HALF, (i + 1) * HALF)
                    sp.dma_start(k_sw[to, a, :, keys], k_st[fro, a, :, keys]).then_inc(k_swapped[2 * i + side], 16)

            def batch(b, first, last):
                if first:
                    sp.wait_ge(w_ready, KT)
                for s in range(SLOTS):
                    unit, of = ended(s, b, first, last)
                    if unit and unit[0] == "qk" and unit[2] < 2:
                        swap(unit, of)
                    for t in range(TILES):
                        if not first and s == PROJ_AT[t][-1] + 4:
                            store(b - 1, t)
                    for t in range(TILES):
                        if not first and s == max(0, PROJ_AT[t][0] - 4):
                            load_res(b - 1, t)
                    if s == PROJ_AT[RING][0]:
                        if not first:
                            sp.wait_ge(done["ht"], count(("ht", TILES - 1), b - 1))
                        for half in range(2):
                            load_x_next(b if last else b + 1, half)

            for t in range(RING):
                sp.dma_start(xt[:, t, :], x_tiles[t]).then_inc(x_loaded[t], 16)
            w_rows = w_qkv.rearrange("(k p) n -> k p n", p=P)
            for k in range(KT):
                sp.dma_start(w_stage[:, k, :], w_rows[k]).then_inc(w_loaded[k], 16)
            for t in range(RING, TILES):
                sp.wait_ge(done["ht"], t - RING + 1)
                sp.dma_start(xt[:, t % RING, :], x_tiles[t]).then_inc(x_loaded[t % RING], 16)
            adj_rows = adj.rearrange("(t p) n -> p t n", p=P)
            for half in range(2):
                tiles = slice(half * TILES // 2, (half + 1) * TILES // 2)
                sp.dma_start(adj_stage[:, tiles, :], adj_rows[:, tiles, :]).then_inc(adj_loaded[half], 16)
            sp.dma_start(wo_stage, w_proj.rearrange("(k p) n -> p k n", p=P)).then_inc(w_out_loaded, 16)
            for row, tile, signal in ((b_proj, bias_b, bias_loaded), (gamma, gamma_b, gamma_loaded),
                                      (beta, beta_b, beta_loaded)):
                sp.dma_start(tile[:], row.rearrange("(a n) -> a n", a=1).broadcast_to([P, D])).then_inc(signal, 16)
            for i in range(2):
                swap(("qk", 0, i), -1)
            run(sp.Fori, batch)
            for t in range(TILES):
                sp.wait_ge(out_ready, (B - 1) * TILES + t + 1)
                sp.dma_start(out_tiles[(B - 1) * TILES + t], x_next[:, t, :]).then_inc(out_stored[t % RING], 16)
            for r in range(RING):
                sp.wait_ge(out_stored[r], 16 * stores(B - 1, RING + r))

        @block.tensor
        def _(pe):
            def scores(b, w, s):
                g = b * SLOTS + w * STEPS + s
                a, h, j = w % 2, s % 2, 2 * (s // 4) + s % 4 // 2
                if s == 0:
                    pe.wait_ge(read["qk"], (b * PAIRS + w) * 4 + 3)
                    for i in range(4):
                        pe.wait_ge(k_swapped[i], 16 * (b * PAIRS + w + 1))
                if s == STEPS // 2:
                    pe.wait_ge(read["qk"], (b * PAIRS + w) * 4 + 4)
                since(pe, exp_ready, g - 1)
                for n in range(2):
                    keys = slice(n * HALF, (n + 1) * HALF)
                    q = q_st[:, a, h, j * P:(j + 1) * P]
                    nc.tensor.matmul(ps_s[:, s % 2, keys], q, k_sw[:, a, h, keys], start=True, stop=False)
                    last = nc.tensor.matmul(ps_s[:, s % 2, keys], q, k_st[:, a, h, keys], start=False, stop=True)
                last.then_inc(scores_ready, 1)

            def transposes(g, parity):
                pe.wait_ge(probs_ready, g + 1)
                for half in range(2):
                    since(pe, pt_ready, 2 * g - 1 + half)
                    for i in range(4):
                        t = half * 4 + i
                        last = nc.tensor.transpose(ps_t[:, half, i, :], probs[:, parity, t * P:(t + 1) * P], ident[:])
                    last.then_inc(transposed, 1)

            def values(b, w, c, part):
                n = (b * PAIRS + w) * CHUNKS + c
                if part == 0:
                    pe.wait_ge(pt_ready, 8 * (n + 1))
                    since(pe, ot_ready, n)
                if c == 0 and w % 2 == 0:
                    pe.wait_ge(read["v"], (b * 2 + w // 2) * 4 + part + 1)
                for t in (2 * part, 2 * part + 1):
                    for h in range(2):
                        col = (w % 2) * P + h * HD
                        last = nc.tensor.matmul(ps_o[h * HD:(h + 1) * HD, :], v[:, w // 2, t, col:col + HD],
                                                pt[:, c % 2, h, t, :], start=(t == 0), stop=(t == TILES - 1))
                if part == 3:
                    last.then_inc(heads_ready, 1)

            def split_matmuls(dst, stationary, moving, tiles):
                for k in tiles:
                    for sa, mo in ((0, 1), (1, 0), (0, 0)):
                        last = nc.tensor.matmul(dst, stationary(k, sa), moving(k, mo), start=(k == 0 and mo == 1),
                                                stop=(k == KT - 1 and sa == mo))
                return last

            def do(unit, part, parts, b, before, bank):
                if before and part == 0:
                    pe.wait_ge(read[before[0][0]], count(*before))
                kind = unit[0]
                w_, wo_, h_, o_ = (w_hi, w_lo), (wo_hi, wo_lo), (ht_hi, ht_lo), (ot_hi, ot_lo)
                if kind in ("qk", "v") and part == 0:
                    there = (b + 1 if for_next(unit) else b) * TILES
                    pe.wait_ge(read["ht"], there + (4 * (unit[2] % 2) + 4 if kind == "qk" else 2 * unit[2] + 2))
                tiles = range(part * KT // parts, (part + 1) * KT // parts)
                if kind == "proj":
                    t = unit[1]
                    if part == 0:
                        pe.wait_ge(ot_ready, ((b - 1) * PAIRS + PAIRS - 1) * CHUNKS + t // 2 + 1)
                    last = split_matmuls(bank, lambda k, e: o_[e][:, k, t * P:(t + 1) * P],
                                         lambda k, e: wo_[e][:, k, :], tiles)
                elif kind == "ht":
                    t = unit[1]
                    pe.wait_ge(h_ready, count(unit, b))
                    for k in range(KT):
                        last = nc.tensor.transpose(bank[:, k * P:(k + 1) * P],
                                                   ln_tile(t, isinstance(b, int) and b < 0)[:, k * P:(k + 1) * P],
                                                   ident[:])
                elif kind == "qk":
                    _, pair, i = unit
                    col = (D if i < 2 else 0) + pair * P
                    rows = slice(i % 2 * HALF, (i % 2 + 1) * HALF)
                    last = split_matmuls(bank, lambda k, e: w_[e][:, k, col:col + P],
                                         lambda k, e: h_[e][:, k, rows], tiles)
                else:
                    _, half, i = unit
                    col = 2 * D + half * 2 * P
                    for e2 in range(2 * part // parts, 2 * (part + 1) // parts):
                        rows = slice((2 * i + e2) * P, (2 * i + e2 + 1) * P)
                        last = split_matmuls(bank[:, e2 * 2 * P:(e2 + 1) * 2 * P],
                                             lambda k, e: h_[e][:, k, rows],
                                             lambda k, e: w_[e][:, k, col:col + 2 * P], range(KT))
                if part == parts - 1:
                    last.then_inc(done[kind], 1)

            def batch(b, first, last):
                before = None if first else (ENDS[SLOTS - 1], b - 1)
                for s in range(SLOTS):
                    g = b * SLOTS + s
                    scores(b, s // STEPS, s % STEPS)
                    if s >= 2 or not first:
                        transposes(g - 2, s % 2)
                    unit, part, parts = FILL[s]
                    if s in EARLY and not last:
                        do(unit, 0, 1, b, before, ps_f[:])
                        before = (unit, b)
                    c, quarter = divmod(s - 6, 4)
                    if c >= 0:
                        values(b, c // CHUNKS, c % CHUNKS, quarter)
                    elif not first:
                        values(b - 1, PAIRS - 1, CHUNKS + c, quarter)
                    if s in EARLY:
                        pass
                    elif first and s in START:
                        do(START[s], 0, 1, -1, before, ps_f[:])
                        before = (START[s], -1)
                    elif has(unit, first, last):
                        do(unit, part, parts, b, before, ps_f[:])
                        if part == parts - 1:
                            before = (unit, b)
                if first:
                    pe.wait_ge(w_ready, KT + 1)

            pe.wait_ge(ident_ready, 1)
            for t in range(TILES):
                before = (("ht", t - len(spare)), -1) if t >= len(spare) else None
                do(("ht", t), 0, 1, -1, before, spare[t % len(spare)])
            for k in range(KT):
                pe.wait_ge(w_ready, k + 1)
                do(("qk", 0, 0), k, KT, -1, None, spare_qk[0])
                if k < KT - 1:
                    do(("qk", 0, 2), k, KT, -1, None, spare_qk[2])
            do(("qk", 0, 1), 0, 1, -1, None, spare_qk[1])
            do(("qk", 0, 2), KT - 1, KT, -1, None, spare_qk[2])
            run(pe.Fori, batch)
            for g in range(B * SLOTS - 2, B * SLOTS):
                transposes(g, g % 2)
            for part in (2, 3):
                values(B - 1, PAIRS - 1, CHUNKS - 2, part)
            for part in range(4):
                values(B - 1, PAIRS - 1, CHUNKS - 1, part)
            for t in range(TILES):
                n = t - len(spare)
                before = (("proj", n), B) if n >= 0 else None
                do(("proj", t), 0, 1, B, before, spare[t % len(spare)])

        @block.vector
        def _(dve):
            def normalise(g, parity):
                dve.wait_ge(exp_ready, g + 1)
                nc.vector.reciprocal(inv_sum[:, parity:parity + 1], row_sum[:, parity:parity + 1]).then_inc(inverted, 1)
                dve.wait_ge(inverted, g + 1)
                nc.vector.tensor_scalar(probs[:, parity, :], probs[:, parity, :], inv_sum[:, parity:parity + 1],
                                        None, ALU.mult).then_inc(probs_ready, 1)

            def mask_and_max(g, s, first_window):
                j = 2 * (s // 4) + s % 4 // 2
                if first_window:
                    dve.wait_ge(mask_ready, j + 1)
                dve.wait_ge(scores_ready, g + 1)
                carry_wait()
                nc.vector.tensor_tensor_reduce(ps_s[:, s % 2, :], ps_s[:, s % 2, :], mask[:, j, :], score_scale[:],
                                               HUGE, ALU.add, ALU.min, neg_max[:, s % 2:s % 2 + 1]).then_inc(masked, 1)

            def low_heads(b, w, c):
                n = (b * PAIRS + w) * CHUNKS + c + 1
                dve.wait_ge(ot_high, n)
                rows = slice(c * 2 * P, (c + 1) * 2 * P)
                nc.vector.tensor_tensor(ot_lo[:, w, rows], ps_o[:], ot_hi[:, w, rows], ALU.subtract).then_inc(ot_ready, 1)

            def take(unit, b, bank):
                kind, n = unit[0], count(unit, b)
                dve.wait_ge(done[kind], n)
                if kind == "proj":
                    t = unit[1]
                    dve.wait_ge(x_plus_o, n)
                    nc.vector.scalar_tensor_tensor(
                        out=o_t[:, t % 2, :], in0=bank, scalar=proj_scale[:].bitcast(F32), in1=bias_b[:],
                        op0=ALU.mult, op1=ALU.add).then_inc(read[kind], 1)
                elif kind == "ht":
                    rows = slice(unit[1] * P, (unit[1] + 1) * P)
                    dve.wait_ge(high[kind], n)
                    nc.vector.scalar_tensor_tensor(
                        out=ht_lo[:, :, rows], in0=bank.rearrange("p (k n) -> p k n", k=KT),
                        scalar=2.0 ** H_SCALE_LOG2, in1=ht_hi[:, :, rows], op0=ALU.mult,
                        op1=ALU.subtract).then_inc(read[kind], 1)
                elif kind == "qk":
                    _, pair, i = unit
                    dst = k_st if i < 2 else q_st
                    rows = slice(i % 2 * HALF, (i % 2 + 1) * HALF)
                    dve.wait_ge(high[kind], n)
                    for h in range(2):
                        here = slice(h * HD, (h + 1) * HD)
                        there = slice((1 - h) * HD, (1 - h) * HD + HD)
                        last = nc.vector.scalar_tensor_tensor(
                            out=dst[there, pair % 2, h, rows], in0=bank[here, :], scalar=OUT_OF_PSUM,
                            in1=dst[here, pair % 2, h, rows], op0=ALU.mult, op1=ALU.subtract)
                    last.then_inc(read[kind], 1)
                else:
                    _, half, i = unit
                    nc.vector.tensor_scalar(v[:, half, 2 * i:2 * i + 2, :], bank.rearrange("p (e n) -> p e n", e=2),
                                            OUT_OF_PSUM, None, ALU.mult).then_inc(read[kind], 1)

            def o_statistics(t, n):
                dve.wait_ge(read["proj"], n)
                nc.vector.bn_stats(o_st[:, t % 2, :], o_t[:, t % 2, :]).then_inc(o_stats, 1)
                dve.wait_ge(o_stats, n)
                carry_wait()
                nc.vector.bn_aggr(o_mv[:, t % 2, :], o_st[:, t % 2, :]).then_inc(o_moments, 1)

            def standardise(b, t):
                n = b * TILES + t + 1
                dve.wait_ge(o_dev, n)
                since(dve, out_ready, n - 1)
                nc.vector.tensor_scalar(norm_t[:], o_t[:, t % 2, :], o_mv[:, t % 2, 0:1], o_aff[:, t % 2, 1:2],
                                        ALU.subtract, ALU.mult).then_inc(o_normed, 1)

            def x_statistics(b, t):
                n = b * TILES + t + 1
                first = isinstance(b, int) and b == 0
                if first:
                    dve.wait_ge(x_loaded[t % RING], 16 * (t // RING + 1))
                else:
                    dve.wait_ge(x_next_loaded[t // (TILES // 2)], 16 * b)
                since(dve, x_affine, n - 2)
                nc.vector.bn_stats(x_st[:, t % 2, :], ln_tile(t, first)).then_inc(x_stats, 1)
                dve.wait_ge(x_stats, n)
                carry_wait()
                nc.vector.bn_aggr(x_mv[:, t % 2, :], x_st[:, t % 2, :]).then_inc(x_moments, 1)

            def batch(b, first, last):
                for s in range(SLOTS):
                    g = b * SLOTS + s
                    unit, of = ended(s, b, first, last)
                    if s % 4 == 2:
                        c = (s - 10) // 4
                        if c >= 0:
                            low_heads(b, c // CHUNKS, c % CHUNKS)
                        elif not first:
                            low_heads(b - 1, PAIRS - 1, CHUNKS + c)
                    if unit:
                        take(unit, of, ps_f[:])
                    mask_and_max(g, s % STEPS, first and s < STEPS)
                    if s > 0 or not first:
                        normalise(g - 1, (s - 1) % 2)
                    if s in EARLY and not last:
                        take(FILL[s][0], b, ps_f[:])
                    if unit and unit[0] == "proj":
                        o_statistics(unit[1], count(unit, of))
                    for t in range(TILES):
                        if not first and s == PROJ_AT[t][-1] + 2:
                            standardise(b - 1, t)
                        if not last and s == STATS_AT[t]:
                            x_statistics(b + 1, t)
                    if first and s == STEPS // 2 - 1:
                        largest_w_proj()
                        nc.vector.sem_inc(w_top_ready, 1)
                    if first and s == STEPS // 2 + 1:
                        scale(1)
                    if first and s == STEPS - 4:
                        low_w_proj()

            steps = [0]

            def prep(instruction):
                instruction.then_inc(w_prep, 1)
                steps[0] += 1
                dve.wait_ge(w_prep, steps[0])

            def largest_w_proj():
                dve.wait_ge(w_out_loaded, 16)
                prep(nc.vector.tensor_scalar(w_abs, wo_stage.rearrange("p k n -> p (k n)").bitcast(I32), 0x7FFFFFFF,
                                             None, ALU.bitwise_and))
                prep(nc.vector.tensor_reduce(w_top[:, 1:2], w_abs.bitcast(F32), AX_X, ALU.max))

            def scale(matrix):
                a = slice(matrix, matrix + 1)
                dve.wait_ge(w_max_ready, matrix + 1)
                prep(nc.vector.tensor_scalar(top_bits[:, a], w_all[:, a].bitcast(I32), 0x7F800000, None,
                                             ALU.bitwise_and))
                prep(nc.vector.tensor_scalar(clamped_bits[:, a], top_bits[:, a], float(80 << MANT), None, ALU.max))
                nc.vector.tensor_scalar(w_scale[:, a], clamped_bits[:, a], -1.0, float((254 + W_TOP_LOG2) << MANT),
                                        ALU.mult, ALU.add).then_inc(scale_ready, 1)
                dve.wait_ge(scale_ready, matrix + 1)

            def low_w_qkv(k):
                dve.wait_ge(w_high, k + 1)
                nc.vector.scalar_tensor_tensor(out=w_lo[:, k, :], in0=w_stage[:, k, :],
                                               scalar=w_scale[:, 0:1].bitcast(F32), in1=w_hi[:, k, :],
                                               op0=ALU.mult, op1=ALU.subtract).then_inc(w_ready, 1)

            def low_w_proj():
                dve.wait_ge(w_high, KT + 1)
                nc.vector.scalar_tensor_tensor(
                    out=wo_lo[:].rearrange("p k n -> p (k n)"), in0=wo_stage.rearrange("p k n -> p (k n)"),
                    scalar=w_scale[:, 1:2].bitcast(F32), in1=wo_hi[:].rearrange("p k n -> p (k n)"),
                    op0=ALU.mult, op1=ALU.subtract).then_inc(w_ready, 1)
                prep(nc.vector.tensor_scalar(product_bits[:, 1:2], clamped_bits[:, 0:1],
                                             -float((127 + 2 * W_TOP_LOG2 + ATT_LOG2) << MANT), None, ALU.add))
                prep(nc.vector.tensor_tensor(proj_scale[:], product_bits[:, 1:2], clamped_bits[:, 1:2], ALU.add))

            x_statistics(0, 0)
            x_statistics(0, 1)
            for k in range(KT):
                dve.wait_ge(w_sized, k + 1)
                prep(nc.vector.tensor_reduce(w_part[:, k:k + 1], w_qkv_abs[k], AX_X, ALU.max))
                x_statistics(0, k + 2)
                take(("ht", k), -1, spare[k % len(spare)])
            prep(nc.vector.tensor_reduce(w_top[:, 0:1], w_part[:], AX_X, ALU.max))
            nc.vector.sem_inc(w_top_ready, 1)
            x_statistics(0, KT + 2)
            scale(0)
            for k in range(KT):
                if k == 0:
                    x_statistics(0, KT + 3)
                take(("ht", KT + k), -1, spare[(KT + k) % len(spare)])
                low_w_qkv(k)
            prep(nc.vector.tensor_scalar(
                product_bits[:, 0:1], clamped_bits[:, 0:1], 2.0,
                -float((127 + 2 * (W_TOP_LOG2 + ATT_LOG2) + ATT_LOG2_SCALE) << MANT), ALU.mult, ALU.add))
            prep(nc.vector.tensor_scalar(score_scale[:], product_bits[:, 0:1].bitcast(F32), -1.0, None, ALU.mult))
            for i in range(3):
                take(("qk", 0, i), -1, spare_qk[i])
            dve.wait_ge(bias_loaded, 16)
            run(dve.Fori, batch)
            normalise(B * SLOTS - 1, 1)
            for c in (CHUNKS - 2, CHUNKS - 1):
                low_heads(B - 1, PAIRS - 1, c)
            for t in range(TILES + 1):
                n = (B - 1) * TILES + t + 1
                if t < TILES:
                    if t >= 2:
                        dve.wait_ge(o_normed, n - 2)
                    take(("proj", t), B, spare[t % len(spare)])
                    o_statistics(t, count(("proj", t), B))
                if t:
                    dve.wait_ge(o_dev, n - 1)
                    dve.wait_ge(x_plus_o, n - 1 + 2)
                    dve.wait_ge(o_normed, n - 1)
                    nc.vector.scalar_tensor_tensor(
                        out=x_next[:, t - 1, :], in0=norm_t[:], scalar=o_aff[:, (t - 1) % 2, 1:2],
                        in1=x_next[:, t - 1, :], op0=ALU.mult, op1=ALU.add).then_inc(out_ready, 1)
                if t < TILES:
                    dve.wait_ge(o_moments, n)
                    dve.wait_ge(out_ready, n - 1)
                    nc.vector.scalar_tensor_tensor(
                        out=norm_t[:], in0=o_t[:, t % 2, :], scalar=o_mv[:, t % 2, 0:1], in1=gamma_b[:],
                        op0=ALU.subtract, op1=ALU.mult).then_inc(o_normed, 1)

        @block.scalar
        def _(act):
            def high_part(unit, b, bank):
                kind, n = unit[0], count(unit, b)
                act.wait_ge(done[kind], n)
                if kind == "ht":
                    rows = slice(unit[1] * P, (unit[1] + 1) * P)
                    nc.scalar.activation(ht_hi[:, :, rows], bank.rearrange("p (k n) -> p k n", k=KT),
                                         ACT.Copy, scale=2.0 ** H_SCALE_LOG2).then_inc(high[kind], 1)
                else:
                    _, pair, i = unit
                    dst = k_st if i < 2 else q_st
                    rows = slice(i % 2 * HALF, (i % 2 + 1) * HALF)
                    for h in range(2):
                        here = slice(h * HD, (h + 1) * HD)
                        last = nc.scalar.activation(dst[here, pair % 2, h, rows], bank[here, :], ACT.Copy,
                                                    scale=OUT_OF_PSUM)
                    last.then_inc(high[kind], 1)

            def copy_transposed(g, s, n):
                if s % 4 == 0:
                    since(act, heads_ready, n - 1)
                if isinstance(n, int) and n < 2 and s % 4 == 0:
                    act.wait_ge(mask_ready, TILES // 2 * (n + 1))
                h, c, col = s % 2, s // 4 % 2, s % 4 // 2 * P
                for half in range(2):
                    act.wait_ge(transposed, 2 * g + half + 1)
                    nc.scalar.activation(pt[:, c, h, half * 4:half * 4 + 4, col:col + P], ps_t[:, half, :, :],
                                         ACT.Copy).then_inc(pt_ready, 1)

            def copy_heads(b, w, c):
                act.wait_ge(heads_ready, (b * PAIRS + w) * CHUNKS + c + 1)
                nc.scalar.activation(ot_hi[:, w, c * 2 * P:(c + 1) * 2 * P], ps_o[:],
                                     ACT.Copy).then_inc(ot_high, 1)

            def exponential(g, parity):
                act.wait_ge(masked, g + 1)
                since(act, transposed, 2 * (g - 1))
                nc.scalar.activation(probs[:, parity, :], ps_s[:, parity, :], ACT.Exp,
                                     bias=neg_max[:, parity:parity + 1], scale=-1.0,
                                     accum_out=row_sum[:, parity:parity + 1]).then_inc(exp_ready, 1)

            def relu_norm(b, t):
                act.wait_ge(x_affine, b * TILES + t + 1)
                tile = ln_tile(t, isinstance(b, int) and b == 0)
                nc.scalar.activation(tile, tile, ACT.Relu,
                                     bias=x_aff[:, t % 2, 3:4], scale=x_aff[:, t % 2, 1:2]).then_inc(h_ready, 1)

            def batch(b, first, last):
                for s in range(SLOTS):
                    g = b * SLOTS + s
                    if s % 4 == 2:
                        c = (s - 10) // 4
                        if c >= 0:
                            copy_heads(b, c // CHUNKS, c % CHUNKS)
                        elif not first:
                            copy_heads(b - 1, PAIRS - 1, CHUNKS + c)
                    unit, of = ended(s, b, first, last)
                    if unit and unit[0] in ("ht", "qk"):
                        high_part(unit, of, ps_f[:])
                    for t in range(TILES):
                        if not last and s == STATS_AT[t] + 3:
                            relu_norm(b + 1, t)
                    if s >= 2 or not first:
                        copy_transposed(g - 2, (s - 2) % STEPS, b * (SLOTS // 4) + (s - 2) // 4)
                    if s in EARLY and not last:
                        high_part(FILL[s][0], b, ps_f[:])
                    exponential(g, s % 2)
                    if first and s == STEPS - 5:
                        act.wait_ge(scale_ready, 2)
                        nc.scalar.activation(wo_hi[:], wo_stage, ACT.Copy,
                                             scale=w_scale[:, 1:2].bitcast(F32)).then_inc(w_high, 1)

            relu_norm(0, 0)
            for t in range(KT):
                act.wait_ge(w_loaded[t], 16)
                nc.scalar.activation(w_qkv_abs[t], w_stage[:, t, :], ACT.Abs).then_inc(w_sized, 1)
                relu_norm(0, t + 1)
                high_part(("ht", t), -1, spare[t % len(spare)])
            act.wait_ge(scale_ready, 1)
            for k in range(KT):
                if KT + k + 1 < TILES:
                    relu_norm(0, KT + k + 1)
                high_part(("ht", KT + k), -1, spare[(KT + k) % len(spare)])
                nc.scalar.activation(w_hi[:, k, :], w_stage[:, k, :], ACT.Copy,
                                     scale=w_scale[:, 0:1].bitcast(F32)).then_inc(w_high, 1)
            for i in range(3):
                high_part(("qk", 0, i), -1, spare_qk[i])
            run(act.Fori, batch)
            for g in range(B * SLOTS - 2, B * SLOTS):
                copy_transposed(g, g % STEPS, g // 4)
            for c in (CHUNKS - 2, CHUNKS - 1):
                copy_heads(B - 1, PAIRS - 1, c)

        @block.gpsimd
        def _(pool):
            def x_scale_and_shift(b, t):
                n, a = b * TILES + t + 1, t % 2
                pool.wait_ge(x_moments, n)
                since(pool, h_ready, n - 2)
                nc.gpsimd.tensor_tensor(x_aff[:, a, 0:1], x_mv[:, a, 1:2], eps[:], ALU.add).then_inc(x_var, 1)
                nc.gpsimd.tensor_tensor(x_aff[:, a, 2:3], x_mv[:, a, 0:1], minus_one[:], ALU.mult).then_inc(x_neg, 1)
                pool.wait_ge(x_var, n)
                nc.gpsimd.tensor_tensor(x_aff[:, a, 1:2], x_aff[:, a, 0:1], minus_half[:], ALU.pow).then_inc(x_dev, 1)
                pool.wait_ge(x_neg, n)
                pool.wait_ge(x_dev, n)
                nc.gpsimd.tensor_tensor(x_aff[:, a, 3:4], x_aff[:, a, 2:3], x_aff[:, a, 1:2],
                                        ALU.mult).then_inc(x_affine, 1)

            def add_beta(b, t):
                n, r = b * TILES + t + 1, t % RING
                pool.wait_ge(x_loaded[r], 16 * res_load(b, t))
                nc.gpsimd.tensor_tensor(xt[:, r, :], xt[:, r, :], beta_b[:], ALU.add).then_inc(x_plus_beta, 1)

            def reciprocal_deviation(b, t):
                n, a = b * TILES + t + 1, t % 2
                pool.wait_ge(o_moments, n)
                nc.gpsimd.tensor_tensor(o_aff[:, a, 0:1], o_mv[:, a, 1:2], eps[:], ALU.add).then_inc(o_var, 1)
                pool.wait_ge(o_var, n)
                nc.gpsimd.tensor_tensor(o_aff[:, a, 1:2], o_aff[:, a, 0:1], minus_half[:], ALU.pow).then_inc(o_dev, 1)

            def add_o(n, tile, a):
                pool.wait_ge(x_plus_beta, n)
                nc.gpsimd.tensor_tensor(tile, tile, o_t[:, a, :], ALU.add).then_inc(x_plus_o, 1)

            def finish(b, t):
                n, r, a = b * TILES + t + 1, t % RING, t % 2
                reciprocal_deviation(b, t)
                add_o(n, xt[:, r, :], a)
                pool.wait_ge(o_normed, n)
                nc.gpsimd.tensor_tensor(norm_t[:], norm_t[:], gamma_b[:], ALU.mult).then_inc(o_gamma, 1)
                pool.wait_ge(o_gamma, n)
                pool.wait_ge(x_plus_o, n + 2)
                nc.gpsimd.tensor_tensor(xt[:, r, :], xt[:, r, :], norm_t[:], ALU.add).then_inc(out_ready, 1)

            def batch(b, first, last):
                if not first:
                    add_beta(b - 1, 0)
                    for t in range(TILES):
                        if t + 1 < TILES:
                            add_beta(b - 1, t + 1)
                        finish(b - 1, t)
                if not last:
                    for t in range(TILES):
                        x_scale_and_shift(b + 1, t)
                else:
                    for t in range(TILES):
                        pool.wait_ge(x_next_loaded[t // (TILES // 2)], 16 * B)
                        nc.gpsimd.tensor_tensor(x_next[:, t, :], x_next[:, t, :], beta_b[:],
                                                ALU.add).then_inc(x_plus_beta, 1)

            nc.gpsimd.memset(ident[:], 0.0).then_inc(zeroed, 1)
            for tile, value in ((minus_half, -0.5), (minus_one, -1.0), (eps, EPS)):
                nc.gpsimd.memset(tile[:], value).then_inc(consts_ready, 1)
            for a in range(2):
                nc.gpsimd.memset(o_t[:, a, :], 0.0).then_inc(x_plus_o, 1)
            pool.wait_ge(zeroed, 1)
            nc.gpsimd.affine_select(out=ident[:], in_=ident[:], compare_op=ALU.not_equal, fill=1.0, base=0,
                                    pattern=[[-1, P]], channel_multiplier=1).then_inc(ident_ready, 1)
            pool.wait_ge(consts_ready, 3)
            for t in range(KT + 2):
                x_scale_and_shift(0, t)
            pool.wait_ge(w_top_ready, 1)
            nc.gpsimd.partition_all_reduce(w_all[:, 0:1], w_top[:, 0:1], P, RMAX).then_inc(w_max_ready, 1)
            for t in range(KT + 2, TILES):
                x_scale_and_shift(0, t)
            for j in range(TILES):
                pool.wait_ge(adj_loaded[j // (TILES // 2)], 16)
                nc.gpsimd.tensor_scalar(mask[:, j, :], adj_stage[:, j, :], 0.0, MASKED, ALU.is_equal,
                                        ALU.mult).then_inc(mask_ready, 1)
            pool.wait_ge(w_top_ready, 2)
            nc.gpsimd.partition_all_reduce(w_all[:, 1:2], w_top[:, 1:2], P, RMAX).then_inc(w_max_ready, 1)
            pool.wait_ge(beta_loaded, 16)
            pool.wait_ge(gamma_loaded, 16)
            run(pool.Fori, batch)
            for t in range(TILES):
                reciprocal_deviation(B - 1, t)
                add_o((B - 1) * TILES + t + 1, x_next[:, t, :], t % 2)


INPUTS = ("x", "adj", "L0_gnn_w_qkv", "L0_gnn_w_proj", "L0_gnn_b_proj", "L0_gnn_ln_gamma", "L0_gnn_ln_beta")


def kernel(**inputs):
    import concourse.bacc as bacc
    from concourse.bass_utils import run_bass_kernel_spmd

    nc = bacc.Bacc("TRN2", target_bir_lowering=False, num_devices=1)
    arrays, args = {}, []
    for name in INPUTS:
        a = np.ascontiguousarray(inputs[name])
        arrays[f"in_{name}"] = a
        args.append(nc.dram_tensor(f"in_{name}", a.shape, mybir.dt.from_np(a.dtype), kind="ExternalInput").ap())
    args.append(nc.dram_tensor("out", (B, N, D), F32, kind="ExternalOutput").ap())
    build(nc, *args)
    r = run_bass_kernel_spmd(nc, [arrays], core_ids=[0])
    return r.results[0]["out"]
```
